# Optimizing a Trainium2 kernel written in Bass

```python
import numpy as np
import jax
import jax.numpy as jnp

def _softmax(x, axis=-1):
    return jax.nn.softmax(x, axis=axis)

def _gelu(x):
    return jax.nn.gelu(x, approximate=True)

def _silu(x):
    return jax.nn.silu(x)

def _sigmoid(x):
    return jax.nn.sigmoid(x)

def _layernorm(x, axis=-1, eps=1e-05):
    m = jnp.mean(x, axis=axis, keepdims=True)
    v = jnp.var(x, axis=axis, keepdims=True)
    return (x - m) / jnp.sqrt(v + eps)

def _scatter_add(tgt, idx, src, axis=0):
    return tgt.at[idx].add(src)

def _segment_sum(src, seg, n):
    return jax.ops.segment_sum(src, seg, n)
kernel_name = 'mk_dlrm_tower_d1_rec_r8_57a5f0'

def setup_inputs(seed: int=0):
    np.random.seed(seed)
    _w = jnp.asarray

    def _rec_inputs():
        import jax
        import jax.numpy as jnp
        _tk = jax.random.key(seed)
        dense_ctx = jax.random.normal(jax.random.fold_in(_tk, 190), (1024, 16), jnp.float32)
        ids = jnp.stack([jax.random.randint(jax.random.fold_in(_tk, 200 + f), (1024,), 0, v, jnp.int32) for f, v in enumerate([1250, 1250, 1250, 12500, 12500, 1000, 12500, 1250, 12500, 12500, 1250, 1250, 12500, 1250, 12500, 1250])], axis=1)
        tbl_0 = 0.05 * jax.random.normal(jax.random.fold_in(_tk, 500 + 0), (1250, 256), jnp.float32)
        tbl_1 = 0.05 * jax.random.normal(jax.random.fold_in(_tk, 500 + 1), (1250, 256), jnp.float32)
        tbl_2 = 0.05 * jax.random.normal(jax.random.fold_in(_tk, 500 + 2), (1250, 256), jnp.float32)
        tbl_3 = 0.05 * jax.random.normal(jax.random.fold_in(_tk, 500 + 3), (12500, 256), jnp.float32)
        tbl_4 = 0.05 * jax.random.normal(jax.random.fold_in(_tk, 500 + 4), (12500, 256), jnp.float32)
        tbl_5 = 0.05 * jax.random.normal(jax.random.fold_in(_tk, 500 + 5), (1000, 256), jnp.float32)
        tbl_6 = 0.05 * jax.random.normal(jax.random.fold_in(_tk, 500 + 6), (12500, 256), jnp.float32)
        tbl_7 = 0.05 * jax.random.normal(jax.random.fold_in(_tk, 500 + 7), (1250, 256), jnp.float32)
        tbl_8 = 0.05 * jax.random.normal(jax.random.fold_in(_tk, 500 + 8), (12500, 256), jnp.float32)
        tbl_9 = 0.05 * jax.random.normal(jax.random.fold_in(_tk, 500 + 9), (12500, 256), jnp.float32)
        tbl_10 = 0.05 * jax.random.normal(jax.random.fold_in(_tk, 500 + 10), (1250, 256), jnp.float32)
        tbl_11 = 0.05 * jax.random.normal(jax.random.fold_in(_tk, 500 + 11), (1250, 256), jnp.float32)
        tbl_12 = 0.05 * jax.random.normal(jax.random.fold_in(_tk, 500 + 12), (12500, 256), jnp.float32)
        tbl_13 = 0.05 * jax.random.normal(jax.random.fold_in(_tk, 500 + 13), (1250, 256), jnp.float32)
        tbl_14 = 0.05 * jax.random.normal(jax.random.fold_in(_tk, 500 + 14), (12500, 256), jnp.float32)
        tbl_15 = 0.05 * jax.random.normal(jax.random.fold_in(_tk, 500 + 15), (1250, 256), jnp.float32)
        _rk = jax.random.fold_in(_tk, 7)
        W_top1 = 0.125 * jax.random.normal(jax.random.fold_in(_tk, 801), (64, 512), jnp.float32)
        W_top2 = 0.0441942 * jax.random.normal(jax.random.fold_in(_tk, 802), (512, 256), jnp.float32)
        W_top3 = 0.0625 * jax.random.normal(jax.random.fold_in(_tk, 803), (256, 1), jnp.float32)
        b_top1 = jnp.zeros((512,), jnp.float32)
        b_top2 = jnp.zeros((256,), jnp.float32)
        return (dense_ctx, ids, tbl_0, tbl_1, tbl_2, tbl_3, tbl_4, tbl_5, tbl_6, tbl_7, tbl_8, tbl_9, tbl_10, tbl_11, tbl_12, tbl_13, tbl_14, tbl_15, W_top1, b_top1, W_top2, b_top2, W_top3)
    dense_ctx, ids, tbl_0, tbl_1, tbl_2, tbl_3, tbl_4, tbl_5, tbl_6, tbl_7, tbl_8, tbl_9, tbl_10, tbl_11, tbl_12, tbl_13, tbl_14, tbl_15, W_top1, b_top1, W_top2, b_top2, W_top3 = _rec_inputs()

    def _L0_rec_setup():
        import jax, jax.numpy as jnp
        import numpy as np
        B, F, E = (512, 16, 256)
        N_LAYERS = 3
        key = jax.random.key(seed)
        k1, k2, k3 = jax.random.split(key, 3)
        x = jax.random.normal(k1, (B, F, E), dtype=jnp.float32)
        Ws = jax.random.normal(k2, (N_LAYERS, F, F * F), dtype=jnp.float32) * 0.05
        bs = jax.random.normal(k3, (N_LAYERS, F), dtype=jnp.float32) * 0.05
        return {'x': x, 'Ws': Ws, 'bs': bs}
    _L0_rec_all = _L0_rec_setup()
    _L0_rec_in = {k: v for k, v in _L0_rec_all.items() if k in ('Ws', 'bs')}
    del _L0_rec_all
    return {'dense_ctx': dense_ctx, 'ids': ids, 'tbl_0': tbl_0, 'tbl_1': tbl_1, 'tbl_2': tbl_2, 'tbl_3': tbl_3, 'tbl_4': tbl_4, 'tbl_5': tbl_5, 'tbl_6': tbl_6, 'tbl_7': tbl_7, 'tbl_8': tbl_8, 'tbl_9': tbl_9, 'tbl_10': tbl_10, 'tbl_11': tbl_11, 'tbl_12': tbl_12, 'tbl_13': tbl_13, 'tbl_14': tbl_14, 'tbl_15': tbl_15, 'W_top1': W_top1, 'b_top1': b_top1, 'W_top2': W_top2, 'b_top2': b_top2, 'W_top3': W_top3, 'L0_rec_Ws': _L0_rec_in['Ws'], 'L0_rec_bs': _L0_rec_in['bs']}

def reference(dense_ctx, ids, tbl_0, tbl_1, tbl_2, tbl_3, tbl_4, tbl_5, tbl_6, tbl_7, tbl_8, tbl_9, tbl_10, tbl_11, tbl_12, tbl_13, tbl_14, tbl_15, W_top1, b_top1, W_top2, b_top2, W_top3, L0_rec_Ws, L0_rec_bs):
    import jax
    import jax.numpy as jnp

    def _L0_rec_ref(x, Ws, bs):
        import jax, jax.numpy as jnp
        import numpy as np
        B, F, E = (512, 16, 256)
        N_LAYERS = 3
        B_, F_, E_ = x.shape
        n_layers = Ws.shape[0]
        xk = x
        outs = []
        for i in range(n_layers):
            z = jnp.einsum('bfe,bge->bfge', x, xk).reshape(B_, F_ * F_, E_)
            z = jnp.swapaxes(z, 1, 2)
            z = jnp.einsum('bcl,oc->bol', z, Ws[i]) + bs[i][None, :, None]
            z = jax.nn.relu(z)
            z = jnp.sum(z, axis=-1)
            outs.append(z)
            xk = jnp.broadcast_to(z[:, :, None], (B_, F_, E_))
        return jnp.concatenate(outs, axis=1)
    e = jnp.stack([tbl_0[ids[:, 0]], tbl_1[ids[:, 1]], tbl_2[ids[:, 2]], tbl_3[ids[:, 3]], tbl_4[ids[:, 4]], tbl_5[ids[:, 5]], tbl_6[ids[:, 6]], tbl_7[ids[:, 7]], tbl_8[ids[:, 8]], tbl_9[ids[:, 9]], tbl_10[ids[:, 10]], tbl_11[ids[:, 11]], tbl_12[ids[:, 12]], tbl_13[ids[:, 13]], tbl_14[ids[:, 14]], tbl_15[ids[:, 15]]], axis=1)
    z = _L0_rec_ref(e, L0_rec_Ws, L0_rec_bs)
    z = z.reshape(z.shape[0], -1)
    h = jnp.concatenate([z, dense_ctx], axis=1)
    h = jnp.maximum(h @ W_top1 + b_top1, 0.0)
    h = jnp.maximum(h @ W_top2 + b_top2, 0.0)
    y = h @ W_top3
    return y

_drawn_inputs = setup_inputs


def setup_inputs(seed=0):
    import zlib

    import numpy as np

    out = dict(_drawn_inputs(seed))
    spreads = {'b_top1': (0.0, 2.0), 'b_top2': (0.0, 2.0)}
    factors = {'dense_ctx': 8.0}
    for name, (base, spread) in spreads.items():
        noise = np.random.default_rng([zlib.crc32(name.encode()), seed]).standard_normal(out[name].shape)
        drawn = base * np.exp(spread * noise) if base else spread * noise
        out[name] = jnp.asarray(drawn.astype(out[name].dtype))
    for name, factor in factors.items():
        out[name] = (out[name] * factor).astype(out[name].dtype)
    return out
```

```python
import concourse.bass as bass
from concourse import mybir
from contextlib import ExitStack


def dlrm_tower(nc, dense_ctx, ids, tables, W_top1, b_top1, W_top2, b_top2, W_top3, layer_W, layer_b, out):
    fp32 = mybir.dt.float32
    i32 = mybir.dt.int32
    ALU = mybir.AluOpType
    ACT = mybir.ActivationFunctionType
    AX = mybir.AxisListType

    B, F = ids.shape
    L, O, E = layer_W.shape
    T = B // 128
    H = E // 128
    HB = H * 128
    D = dense_ctx.shape[1]
    C1 = W_top1.shape[1] // 128
    C2 = W_top2.shape[1] // 128
    KIN = L * O + D
    G8 = 128 // O
    NP = F // 2

    POOL_ROWS = [(0, 1, 15), (1, 2, 14), (2, 3, 13), (13, 14, 2)]
    VEC_FIELDS = [14, 12, 11, 10, 9, 8, 7, 6, 5, 4, 3]
    QUAD = 4
    RING_1 = 36
    RING = 40
    vec_segments = []
    at = 0
    for f in VEC_FIELDS:
        g, left = f + 1, F - 1 - f
        while left:
            n = min(left, RING_1 - at) if at < RING_1 else left
            vec_segments.append((f, g, n, at if at < RING_1 else at - RING_1, at))
            g, left, at = g + n, left - n, at + n
    VEC_PAIRS = at
    POOL_PAIRS = sum(n for _, _, n in POOL_ROWS)
    assert VEC_PAIRS + POOL_PAIRS == F * (F - 1) // 2 and VEC_PAIRS - RING_1 == RING
    NV = len(vec_segments)
    NPOOL = len(POOL_ROWS)
    VQ, PQ = VEC_PAIRS // QUAD, POOL_PAIRS // QUAD
    SETS = {0: [("v", q) for q in range(0, 4)], 1: [("v", q) for q in range(4, 8)],
            2: [("d", q) for q in range(4)],
            3: [("v", q) for q in range(8, 12)], 4: [("v", q) for q in range(12, 16)],
            6: [("p", q) for q in range(0, 4)], 7: [("p", q) for q in range(4, 8)],
            8: [("v", q) for q in range(16, VQ)] + [("p", 8)], 9: [("p", q) for q in range(9, PQ)]}
    PROJ = 5
    USES = 10
    ORDER = sorted(SETS)
    NS = len(ORDER)
    SQUARES = 2
    FPS = F // SQUARES
    OPERANDS = [7, 6, 5, 4, 3, 2, 1]
    NOP = len(OPERANDS)

    def set_pairs(u):
        return QUAD * len(SETS[u]) // 4

    def last_segment(f_list):
        return max(i for i, s in enumerate(vec_segments) if s[0] in f_list)

    freed_after = [last_segment([f for f in VEC_FIELDS if f // 2 == n]) + 1 for n in OPERANDS]

    def segments_before_quad(q):
        need = QUAD * (q + 1)
        return min(i for i, s in enumerate(vec_segments) if s[4] + s[2] >= need) + 1

    def pool_rows_before_quad(q):
        total = 0
        for i, (_, _, n) in enumerate(POOL_ROWS):
            total += n
            if total >= QUAD * (q + 1):
                return i + 1

    def ring_guard(seg):
        _, _, n, slot, number = seg
        first_turn = number < RING_1
        readers = []
        for u, quads in SETS.items():
            for kind, q in quads:
                if kind != "v":
                    continue
                for s in range(QUAD * q, QUAD * q + QUAD):
                    turn1 = s < RING_1
                    if turn1 != first_turn and slot <= (s if turn1 else s - RING_1) < slot + n:
                        readers.append(u)
        return (1 if first_turn else 0), max(readers) if readers else None

    CH = 4
    GC = F // CH
    CW = GC * F * O

    ctx = ExitStack()
    with ctx:
        def sb(name, shape, dt=fp32):
            return ctx.enter_context(nc.sbuf_tensor(name, shape, dt))

        def ps(name, shape):
            return ctx.enter_context(nc.psum_tensor(name, shape, fp32))

        def sem(name):
            return ctx.enter_context(nc.semaphore(name))

        ids_sb = sb("ids_sb", [128, 2, F], i32)
        X = [sb(f"X{p}", [128, F, E]) for p in range(2)]
        XT = [sb(f"XT{p}", [128, F, HB]) for p in range(2)]
        vec_pairs = sb("vec_pairs", [128, RING, HB])
        pool_pairs = sb("pool_pairs", [128, POOL_PAIRS, HB])
        squares = sb("squares", [128, F, HB])
        relued = sb("relued", [128, 2, 512])
        partial = sb("partial", [128, 4, 128])
        proj = sb("proj", [128, 2, F * O])
        cross = sb("cross", [128, CH, CW])
        chunk_sums = sb("chunk_sums", [128, CH, O])
        z_group = sb("z_group", [128, 2, O])
        z_spread = sb("z_spread", [128, 2, O, O])
        z_rows = sb("z_rows", [128, 2, G8, O])
        mlp_in = [sb(f"mlp_in{p}", [128, KIN]) for p in range(2)]
        mlp_inT = sb("mlp_inT", [KIN, 128])
        hidden1 = sb("hidden1", [128, C1, 128])
        hidden2 = sb("hidden2", [128, C2, 128])
        tick_word = sb("tick_word", [1, 1])
        y_row = sb("y_row", [1, 2, 128])
        ident = sb("ident", [128, 128])
        pick_in_group = sb("pick_in_group", [128, O])
        group_of = sb("group_of", [128, G8])
        same_group = sb("same_group", [128, G8, O])
        pick_in_32 = sb("pick_in_32", [128, 32])
        place = sb("place", [128, 2, KIN])
        spread16 = sb("spread16", [O, G8, O])
        spread32 = sb("spread32", [O, 4, 32])
        layer_rows = sb("layer_rows", [L * O, E])
        bias_in = sb("bias_in", [O, L])
        WT = sb("WT", [128, L, H, 48])
        bias = sb("bias", [128, 4])
        w1 = sb("w1", [KIN, C1, 128])
        w2 = sb("w2", [128, C1, C2 * 128])
        w3 = sb("w3", [128, C2])
        b1 = sb("b1", [128, C1])
        b2 = sb("b2", [128, C2])

        turn_bank = [ps(f"turn_bank{i}", [128, 512]) for i in range(2)]
        operand_bank = [ps(f"operand_bank{i}", [128, 512]) for i in range(2)]
        work_bank = [ps(f"work_bank{i}", [128, 512]) for i in range(2)]
        sum_bank = ps("sum_bank", [128, 512])
        misc_bank = ps("misc_bank", [128, 512])
        z_everywhere = misc_bank[:, 0:256]
        z0_ps = misc_bank[:, 256:256 + O]
        mlp_inT_ps = misc_bank[0:KIN, 288:288 + 128]

        ids_in = [sem(f"ids_in{p}") for p in range(2)]
        dense_in = [sem(f"dense_in{p}") for p in range(2)]
        y_out = [sem(f"y_out{p}") for p in range(2)]
        gathered = [sem(f"gathered{f}") for f in range(F)]
        weights_in = sem("weights_in")
        mlp_weights_in = sem("mlp_weights_in")
        tick = sem("tick")
        const_pool = sem("const_pool")
        const_vec = sem("const_vec")
        setup_vec = sem("setup_vec")
        setup_pe = sem("setup_pe")
        setup_act = sem("setup_act")
        turned = sem("turned")
        xt_ready = sem("xt_ready")
        operand_ready = sem("operand_ready")
        vec_done = sem("vec_done")
        pool_done = sem("pool_done")
        squared = sem("squared")
        work_filled = sem("work_filled")
        work_drained = sem("work_drained")
        set_summed = sem("set_summed")
        sums_copied = sem("sums_copied")
        z0_ready = sem("z0_ready")
        z0_kept = sem("z0_kept")
        z_spread_done = sem("z_spread_done")
        z_ready = sem("z_ready")
        crossed = sem("crossed")
        cross_relued = sem("cross_relued")
        cross_reduced = sem("cross_reduced")
        z_done = sem("z_done")
        z_rows_done = sem("z_rows_done")
        mlp_pe = sem("mlp_pe")
        mlp_act = sem("mlp_act")
        MA = C1 + C2 + 2

        block = ctx.enter_context(nc.Block())
        OUT_W = slice(16, 32)

        def steps(step):
            step(0, 0, True, True, False)
            with nc_loop[0](0, (T - 2) // 2) as i:
                step(2 * i + 1, 1, True, True, True)
                step(2 * i + 2, 0, True, True, True)
            step(T - 1, 1, True, False, True)
            step(T, 0, False, False, True)

        nc_loop = [None]

        def uses_of_parity(t, p):
            return (t - p) // 2

        @block.sync
        def _(sp):
            def fetch(t, p, k):
                rows = bass.ds(t * 128, 128)
                if not isinstance(k, int) or k > 0:
                    sp.wait_ge(turned, NP * (t - 1))
                sp.dma_start(ids_sb[:, p, :], ids[rows, :]).then_inc(ids_in[p], 16)
                if not isinstance(k, int) or k > 0:
                    sp.wait_ge(mlp_pe, 4 * (t - 2) + 1)
                sp.dma_start(mlp_in[p][:, L * O:KIN], dense_ctx[rows, :]).then_inc(dense_in[p], 16)

            def store(t, p):
                sp.wait_ge(mlp_act, MA * (t + 1))
                sp.dma_start(out[bass.ds(t * 128, 128), :].rearrange("b o -> o b"),
                             y_row[0:1, p, :]).then_inc(y_out[p], 16)

            fetch(0, 0, 0)
            sp.dma_start(layer_rows[:, :], layer_W.rearrange("l o e -> (l o) e")).then_inc(weights_in, 16)
            with nc.allow_non_contiguous_dma(reason="48 biases, once"):
                sp.dma_start(bias_in[:, :], layer_b.rearrange("l o -> o l")).then_inc(weights_in, 16)
            fetch(1, 1, 0)
            sp.dma_start(w1[:, :, :], W_top1.rearrange("k (c n) -> k c n", n=128)).then_inc(mlp_weights_in, 16)
            sp.dma_start(w2[:, :, :], W_top2.rearrange("(c k) n -> k c n", k=128)).then_inc(mlp_weights_in, 16)
            with nc.allow_non_contiguous_dma(reason="768 biases and 256 weights, once"):
                sp.dma_start(w3[:, :], W_top3.rearrange("(c k) o -> k (c o)", k=128)).then_inc(mlp_weights_in, 16)
                sp.dma_start(b1[:, :], b_top1.rearrange("(c k) -> k c", k=128)).then_inc(mlp_weights_in, 16)
                sp.dma_start(b2[:, :], b_top2.rearrange("(c k) -> k c", k=128)).then_inc(mlp_weights_in, 16)
            with sp.Fori(0, (T - 2) // 2) as i:
                fetch(2 * i + 2, 0, i + 1)
                store(2 * i, 0)
                fetch(2 * i + 3, 1, i + 1)
                store(2 * i + 1, 1)
            store(T - 2, 0)
            store(T - 1, 1)
            for p in range(2):
                sp.wait_ge(y_out[p], 16 * (T // 2))

        @block.gpsimd
        def _(pool):
            def gathers(t, p, k):
                pool.wait_ge(ids_in[p], 16 * (k + 1))
                if not isinstance(k, int) or k > 0:
                    pool.wait_ge(operand_ready, NOP * (t - 1))
                    pool.wait_ge(turned, NP * (t - 1))
                if not (isinstance(t, int) and t == 0):
                    for f in range(F):
                        pool.wait_ge(gathered[f], 16 * t)
                if not (isinstance(t, int) and t == 0):
                    pool.wait_ge(const_pool, 2)
                    pool.wait_ge(tick, t - 1)
                    pool.tensor_tensor(tick_word[:, :], ident[0:1, 0:1], ident[0:1, 0:1],
                                       ALU.mult).then_inc(tick, 1)
                for f in reversed(range(F)):
                    pool.indirect_dma_start(
                        X[p][:, f, :], None, tables[f][:, :],
                        bass.IndirectOffsetOnAxis(ap=ids_sb[:, p, f:f + 1], axis=0)).then_inc(gathered[f], 16)

            def pairs(t, p):
                at = 0
                pool.wait_ge(xt_ready, NP * (t + 1))
                if not (isinstance(t, int) and t == 0):
                    pool.wait_ge(work_filled, USES * t)
                for f, g, n in POOL_ROWS:
                    pool.tensor_tensor(pool_pairs[:, at:at + n, :],
                                       XT[p][:, f:f + 1, :].to_broadcast([128, n, HB]),
                                       XT[p][:, g:g + n, :], ALU.mult).then_inc(pool_done, 1)
                    at += n

            pool.memset(ident[:, :], 0.0).then_inc(const_pool, 1)
            gathers(0, 0, 0)
            pool.wait_ge(const_pool, 1)
            pool.affine_select(out=ident[:, :], in_=ident[:, :], compare_op=ALU.not_equal, fill=1.0,
                               base=0, pattern=[[-1, 128]], channel_multiplier=1).then_inc(const_pool, 1)
            gathers(1, 1, 0)
            pairs(0, 0)
            with pool.Fori(0, (T - 2) // 2) as i:
                gathers(2 * i + 2, 0, i + 1)
                pairs(2 * i + 1, 1)
                gathers(2 * i + 3, 1, i + 1)
                pairs(2 * i + 2, 0)
            pairs(T - 1, 1)

        @block.scalar
        def _(act):
            def turn_copy(t, p, n, first=False):
                m = NP - 1 - n
                act.wait_ge(turned, NP * t + m + 1)
                if m == 0 and not first:
                    act.wait_ge(vec_done, NV * (t - 1))
                    act.wait_ge(pool_done, NPOOL * (t - 1))
                    act.wait_ge(squared, SQUARES * (t - 1))
                    act.wait_ge(work_filled, USES * (t - 2) + PROJ + 1)
                act.activation(XT[p][:, 2 * n:2 * n + 2, :], turn_bank[m % 2][:, :], ACT.Copy).then_inc(xt_ready, 1)

            def square(t, p, i, first):
                if i == 0:
                    act.wait_ge(xt_ready, NP * (t + 1))
                    if not first:
                        act.wait_ge(work_filled, USES * (t - 1) + 3)
                act.activation(squares[:, i * FPS:(i + 1) * FPS, :], XT[p][:, i * FPS:(i + 1) * FPS, :],
                               ACT.Square).then_inc(squared, 1)

            def relu_set(t, u, first):
                s = ORDER.index(u)
                act.wait_ge(work_filled, USES * t + u + 1)
                if not (first and s < 2):
                    act.wait_ge(set_summed, NS * t + s - 1)
                cols = 128 * set_pairs(u)
                twice = u != 2
                act.activation(relued[:, s % 2, 0:cols], work_bank[u % 2][:, 0:cols], ACT.Relu,
                               bias=bias[:, 3:4] if twice else bias[:, 2:3],
                               scale=2.0 if twice else 1.0).then_inc(work_drained, 1)

            def copy_sums(t):
                act.wait_ge(set_summed, NS * (t + 1))
                act.activation(partial[:, :, :], sum_bank[:, :], ACT.Copy).then_inc(sums_copied, 1)

            def copy_proj(t, first):
                act.wait_ge(work_filled, USES * t + PROJ + 1)
                if not first:
                    act.wait_ge(crossed, 2 * CH * t)
                act.activation(proj[:, :, :], work_bank[PROJ % 2][:, :], ACT.Copy).then_inc(work_drained, 1)

            def relu_cross(t, l):
                for c in range(CH):
                    act.wait_ge(crossed, 2 * CH * t + CH * l + c + 1)
                    act.activation(cross[:, c, :], cross[:, c, :], ACT.Relu,
                                   bias=bias[:, l:l + 1]).then_inc(cross_relued, 1)

            def mlp(t, p):
                act.wait_ge(mlp_pe, 4 * t + 1)
                act.activation(mlp_inT[:, :], mlp_inT_ps, ACT.Copy).then_inc(mlp_act, 1)
                act.wait_ge(mlp_pe, 4 * t + 2)
                for c in range(C1):
                    act.activation(hidden1[:, c, :], turn_bank[0][:, c * 128:(c + 1) * 128], ACT.Relu,
                                   bias=b1[:, c:c + 1]).then_inc(mlp_act, 1)
                act.wait_ge(mlp_pe, 4 * t + 3)
                for c in range(C2):
                    act.activation(hidden2[:, c, :], turn_bank[1][:, c * 128:(c + 1) * 128], ACT.Relu,
                                   bias=b2[:, c:c + 1]).then_inc(mlp_act, 1)
                act.wait_ge(mlp_pe, 4 * t + 4)
                act.wait_ge(y_out[p], 16 * uses_of_parity(t, p))
                act.activation(y_row[0:1, p, :], turn_bank[1][0:1, 256:384], ACT.Copy).then_inc(mlp_act, 1)

            def step(t, p, front, fetch, back):
                first = isinstance(t, int) and t == 0
                q = 1 - p
                if back:
                    copy_sums(t - 1)
                if front:
                    square(t, p, 0, first)
                if back:
                    relu_cross(t - 1, 0)
                if front:
                    relu_set(t, 0, first)
                if fetch:
                    if first:
                        turn_copy(t + 1, q, 7, True)
                    else:
                        turn_copy(t + 1, q, 7)
                    turn_copy(t + 1, q, 6)
                if front:
                    relu_set(t, 1, first)
                    square(t, p, 1, first)
                    relu_set(t, 2, first)
                if fetch:
                    turn_copy(t + 1, q, 5)
                    turn_copy(t + 1, q, 4)
                if back:
                    relu_cross(t - 1, 1)
                if front:
                    relu_set(t, 3, first)
                    relu_set(t, 4, first)
                if fetch:
                    turn_copy(t + 1, q, 3)
                    turn_copy(t + 1, q, 2)
                if front:
                    copy_proj(t, first)
                    relu_set(t, 6, first)
                if fetch:
                    turn_copy(t + 1, q, 1)
                    turn_copy(t + 1, q, 0)
                if back:
                    mlp(t - 1, q)
                if front:
                    for u in (7, 8, 9):
                        relu_set(t, u, first)

            act.wait_ge(setup_pe, 1)
            for h in range(H):
                act.activation(WT[:, :, h, OUT_W],
                               work_bank[0][:, 48 * h:48 * h + 48].rearrange("p (l o) -> p l o", l=L),
                               ACT.Copy).then_inc(setup_act, 1)
            act.activation(bias[:, 0:3], work_bank[0][:, 128:131], ACT.Copy).then_inc(setup_act, 1)
            act.activation(bias[:, 3:4], work_bank[0][:, 130:131], ACT.Copy, scale=2.0).then_inc(setup_act, 1)
            act.wait_ge(setup_act, 4)
            act.wait_ge(const_vec, 1)
            act.wait_ge(mlp_weights_in, 80)
            for n in reversed(range(NP)):
                turn_copy(0, 0, n, True)
            nc_loop[0] = act.Fori
            steps(step)

        @block.tensor
        def _(pe):
            def turn(t, p, n, first=False):
                m = NP - 1 - n
                for f in (2 * n + 1, 2 * n):
                    pe.wait_ge(gathered[f], 16 * (t + 1))
                if not (first and m < 2):
                    pe.wait_ge(xt_ready, NP * t + m - 1)
                if m < 2 and not first and not (isinstance(t, int) and t <= 1):
                    pe.wait_ge(mlp_act, MA * (t - 2))
                for i in range(2):
                    for h in range(H):
                        last = pe.transpose(turn_bank[m % 2][:, 256 * i + 128 * h:256 * i + 128 * h + 128],
                                            X[p][:, 2 * n + i, 128 * h:128 * h + 128], ident[:, :])
                last.then_inc(turned, 1)

            def operand(t, p, m, first=False):
                n = OPERANDS[m]
                if m >= 2:
                    pe.wait_ge(vec_done, NV * t + freed_after[m - 2])
                elif not first:
                    pe.wait_ge(vec_done, NV * (t - 1) + freed_after[NOP - 1 - m])
                for f in (2 * n, 2 * n + 1):
                    pe.wait_ge(gathered[f], 16 * (t + 1))
                for i in range(2):
                    for h in range(H):
                        last = pe.transpose(operand_bank[m % 2][:, 256 * i + 128 * h:256 * i + 128 * h + 128],
                                            X[p][:, 2 * n + i, 128 * h:128 * h + 128], ident[:, :])
                last.then_inc(operand_ready, 1)

            def wait_work_bank(t, u, first):
                if not (first and u < 2):
                    pe.wait_ge(work_drained, USES * t + u - 1)

            def contract(t, u, first):
                wait_work_bank(t, u, first)
                for kind, q in SETS[u][-1:] if u in (6, 7, 9) else SETS[u]:
                    if kind == "p":
                        pe.wait_ge(pool_done, NPOOL * t + pool_rows_before_quad(q))
                    elif kind == "v" and (kind, q) == [s for s in SETS[u] if s[0] == "v"][-1]:
                        pe.wait_ge(vec_done, NV * t + segments_before_quad(q))
                    elif kind == "d" and q == 0:
                        pe.wait_ge(squared, SQUARES * (t + 1))
                for h in range(H):
                    n = set_pairs(u)
                    for j in range(4):
                        kind, q = SETS[u][n * j // QUAD]
                        slot = QUAD * q + n * j % QUAD
                        if kind == "v" and slot >= RING_1:
                            slot -= RING_1
                        src = {"v": vec_pairs, "p": pool_pairs, "d": squares}[kind]
                        last = pe.matmul(work_bank[u % 2][32 * j:32 * j + 32, 0:128 * n], WT[:, 0, h, 16:48],
                                         src[:, slot:slot + n, 128 * h:128 * h + 128],
                                         start=(h == 0), stop=(h == H - 1))
                last.then_inc(work_filled, 1)

            def add_set(t, u, first):
                s = ORDER.index(u)
                pe.wait_ge(work_drained, USES * t + u + 1)
                if s == 0 and not first:
                    pe.wait_ge(sums_copied, t)
                j = s % 4
                cols = 128 * set_pairs(u)
                pe.matmul(sum_bank[32 * j:32 * j + 32, 0:cols], pick_in_32[:, :], relued[:, s % 2, 0:cols],
                          start=(s < 4), stop=(s + 4 >= NS)).then_inc(set_summed, 1)

            def project(t, p, first):
                wait_work_bank(t, PROJ, first)
                for l in range(2):
                    for k in range(2):
                        for h in range(H):
                            for j in range(4):
                                grp = 2 * j + k
                                last = pe.matmul(
                                    work_bank[PROJ % 2][32 * j:32 * j + 32, 256 * l:256 * l + 256],
                                    WT[:, l + 1, h, 16 - 16 * k:48 - 16 * k] if k else WT[:, l + 1, h, 16:48],
                                    XT[p][:, :, 128 * h + O * grp:128 * h + O * grp + O],
                                    start=(k == 0 and h == 0), stop=(k == 1 and h == H - 1))
                last.then_inc(work_filled, 1)

            def finish_z0(t):
                pe.wait_ge(sums_copied, t + 1)
                pe.wait_ge(z0_kept, t)
                pe.wait_ge(z_spread_done, 2 * t)
                for k in range(4):
                    last = pe.matmul(z0_ps, partial[:, k, :], pick_in_32[:, 0:O], start=(k == 0), stop=(k == 3))
                last.then_inc(z0_ready, 1)

            def spread_z(t, l):
                pe.wait_ge(z_spread_done, 2 * t + l + 1)
                pe.wait_ge(crossed, 2 * CH * t + CH * l)
                pe.matmul(z_everywhere, same_group[:, :, :], z_spread[:, l, :, :],
                          start=True, stop=True).then_inc(z_ready, 1)

            def mlp(t, p):
                pe.wait_ge(z0_kept, t + 1)
                pe.wait_ge(dense_in[p], 16 * (uses_of_parity(t, p) + 1))
                pe.wait_ge(z_rows_done, 2 * (t + 1))
                pe.wait_ge(mlp_act, MA * t)
                pe.matmul(mlp_inT_ps, mlp_in[p][:, :], ident[:, :], start=True, stop=False)
                for l in range(2):
                    last = pe.matmul(mlp_inT_ps, place[:, l, :], z_rows[:, l, :, :], start=False, stop=(l == 1))
                last.then_inc(mlp_pe, 1)
                pe.wait_ge(mlp_act, MA * t + 1)
                if isinstance(t, int) and t >= T - 2:
                    pe.wait_ge(xt_ready, NP * T)
                else:
                    pe.wait_ge(xt_ready, NP * (t + 3))
                for c in range(C1):
                    last = pe.matmul(turn_bank[0][:, c * 128:(c + 1) * 128], w1[:, c, :], mlp_inT[:, :],
                                     start=True, stop=True)
                last.then_inc(mlp_pe, 1)
                pe.wait_ge(mlp_act, MA * t + 1 + C1)
                for m in range(C2):
                    for c in range(C1):
                        last = pe.matmul(turn_bank[1][:, m * 128:(m + 1) * 128], w2[:, c, m * 128:(m + 1) * 128],
                                         hidden1[:, c, :], start=(c == 0), stop=(c == C1 - 1))
                last.then_inc(mlp_pe, 1)
                pe.wait_ge(mlp_act, MA * t + 1 + C1 + C2)
                for m in range(C2):
                    last = pe.matmul(turn_bank[1][0:1, 256:384], w3[:, m:m + 1], hidden2[:, m, :],
                                     start=(m == 0), stop=(m == C2 - 1))
                last.then_inc(mlp_pe, 1)

            def step(t, p, front, fetch, back):
                first = isinstance(t, int) and t == 0
                q = 1 - p
                if front:
                    operand(t, p, 2)
                    operand(t, p, 3)
                if back:
                    finish_z0(t - 1)
                if front:
                    operand(t, p, 4)
                if back:
                    spread_z(t - 1, 0)
                if front:
                    operand(t, p, 5)
                    contract(t, 0, first)
                if fetch:
                    turn(t + 1, q, 7)
                    turn(t + 1, q, 6)
                if front:
                    contract(t, 1, first)
                    add_set(t, 0, first)
                if back:
                    spread_z(t - 1, 1)
                if front:
                    contract(t, 2, first)
                    add_set(t, 1, first)
                    operand(t, p, 6)
                if fetch:
                    turn(t + 1, q, 5)
                    turn(t + 1, q, 4)
                if front:
                    contract(t, 3, first)
                    add_set(t, 2, first)
                    contract(t, 4, first)
                    add_set(t, 3, first)
                if fetch:
                    turn(t + 1, q, 3)
                    turn(t + 1, q, 2)
                if front:
                    project(t, p, first)
                    add_set(t, 4, first)
                    contract(t, 6, first)
                if fetch:
                    turn(t + 1, q, 1)
                    turn(t + 1, q, 0)
                    operand(t + 1, q, 0)
                    operand(t + 1, q, 1)
                if back:
                    mlp(t - 1, q)
                if front:
                    for u in (7, 8, 9):
                        contract(t, u, first)
                        add_set(t, ORDER[ORDER.index(u) - 1], first)
                    add_set(t, 9, first)

            pe.wait_ge(const_pool, 2)
            pe.wait_ge(const_vec, 1)
            pe.wait_ge(weights_in, 32)
            for h in range(H):
                pe.transpose(work_bank[0][:, 48 * h:48 * h + 48], layer_rows[:, 128 * h:128 * h + 128],
                             ident[0:L * O, 0:L * O])
            pe.matmul(work_bank[0][:, 128:130], spread16[:, :, :], bias_in[:, 1:3], start=True, stop=True)
            pe.matmul(work_bank[0][:, 130:131], spread32[:, :, :], bias_in[:, 0:1], start=True,
                      stop=True).then_inc(setup_pe, 1)
            pe.wait_ge(setup_act, 4)
            turn(0, 0, 7, True)
            operand(0, 0, 0, True)
            turn(0, 0, 6, True)
            operand(0, 0, 1, True)
            for n in reversed(range(NP - 2)):
                turn(0, 0, n, True)
            pe.wait_ge(mlp_weights_in, 80)
            nc_loop[0] = pe.Fori
            steps(step)

        @block.vector
        def _(vec):
            def segments(t, p, fields, first):
                for i, seg in enumerate(vec_segments):
                    f, g, n, slot, _ = seg
                    if f not in fields:
                        continue
                    m = OPERANDS.index(f // 2)
                    vec.wait_ge(operand_ready, NOP * t + m + 1)
                    vec.wait_ge(xt_ready, NP * t + NP - (g // 2))
                    back, use = ring_guard(seg)
                    if use is not None and not (first and back):
                        vec.wait_ge(work_filled, USES * (t - back) + use + 1)
                    col = 256 * (f % 2)
                    vec.tensor_tensor(vec_pairs[:, slot:slot + n, :],
                                      operand_bank[m % 2][:, None, col:col + HB].to_broadcast([128, n, HB]),
                                      XT[p][:, g:g + n, :], ALU.mult).then_inc(vec_done, 1)

            def keep_z0(t, p):
                vec.wait_ge(z0_ready, t + 1)
                vec.wait_ge(mlp_pe, 4 * t)
                vec.tensor_copy(mlp_in[p][:, 0:O], z0_ps).then_inc(z0_kept, 1)

            def spread(t, l):
                vec.wait_ge(z_ready, 2 * t)
                if l == 0:
                    vec.wait_ge(z0_ready, t + 1)
                    vec.tensor_tensor(z_spread[:, 0, :, :], z0_ps[:, :, None].to_broadcast([128, O, O]),
                                      pick_in_group[:, None, :].to_broadcast([128, O, O]),
                                      ALU.mult).then_inc(z_spread_done, 1)
                else:
                    vec.wait_ge(z_done, 2 * t + 1)
                    vec.tensor_tensor(z_spread[:, 1, :, :], z_group[:, 0:1, :].to_broadcast([128, O, O]),
                                      pick_in_group[:, :, None].to_broadcast([128, O, O]),
                                      ALU.mult).then_inc(z_spread_done, 1)

            def cross_products(t, l):
                vec.wait_ge(z_ready, 2 * t + l + 1)
                vec.wait_ge(work_drained, USES * t + PROJ + 1)
                z = z_everywhere.rearrange("p (g b) -> p g b", b=O)
                P = proj[:, l, :].rearrange("p (f b) -> p f b", b=O)
                for c in range(CH):
                    vec.wait_ge(cross_reduced, 2 * CH * t + (c + 1 if l else 0))
                    vec.tensor_tensor(cross[:, c, :].rearrange("p (g f b) -> p g f b", g=GC, f=F),
                                      z[:, GC * c:GC * c + GC, None, :].to_broadcast([128, GC, F, O]),
                                      P[:, None, :, :].to_broadcast([128, GC, F, O]),
                                      ALU.mult).then_inc(crossed, 1)

            def cross_sums(t, l):
                for c in range(CH):
                    vec.wait_ge(cross_relued, 2 * CH * t + CH * l + c + 1)
                    if c == 0:
                        vec.wait_ge(z_done, 2 * t + l)
                    vec.tensor_reduce(chunk_sums[:, c, :], cross[:, c, :].rearrange("p (x b) -> p b x", b=O),
                                      AX.X, ALU.add).then_inc(cross_reduced, 1)
                vec.wait_ge(cross_reduced, 2 * CH * t + CH * (l + 1))
                vec.wait_ge(z_rows_done, 2 * t)
                vec.tensor_reduce(z_group[:, l, :], chunk_sums[:, :, :].rearrange("p c b -> p b c"),
                                  AX.X, ALU.add).then_inc(z_done, 1)

            def rows_for_mlp(t):
                vec.wait_ge(z_done, 2 * (t + 1))
                vec.wait_ge(mlp_pe, 4 * t)
                for l in range(2):
                    vec.tensor_tensor(z_rows[:, l, :, :], z_group[:, l:l + 1, :].to_broadcast([128, G8, O]),
                                      same_group[:, :, :], ALU.mult).then_inc(z_rows_done, 1)

            def step(t, p, front, fetch, back):
                first = isinstance(t, int) and t == 0
                if front:
                    segments(t, p, (14, 12, 11, 10), first)
                if back:
                    keep_z0(t - 1, 1 - p)
                    spread(t - 1, 0)
                if front:
                    segments(t, p, (9, 8), first)
                if back:
                    cross_products(t - 1, 0)
                if front:
                    segments(t, p, (7,), first)
                if back:
                    cross_sums(t - 1, 0)
                    spread(t - 1, 1)
                if front:
                    segments(t, p, (6, 5), first)
                if back:
                    cross_products(t - 1, 1)
                if front:
                    segments(t, p, (4, 3), first)
                if back:
                    cross_sums(t - 1, 1)
                    rows_for_mlp(t - 1)

            vec.memset(WT[:, :, :, :], 0.0).then_inc(setup_vec, 1)
            for p in range(2):
                vec.memset(mlp_in[p][:, 0:L * O], 0.0).then_inc(setup_vec, 1)
            vec.memset(place[:, :, :], 0.0).then_inc(setup_vec, 1)
            vec.wait_ge(const_pool, 2)
            vec.tensor_reduce(pick_in_group[:, :], ident[:, :].rearrange("p (g c) -> p c g", c=O),
                              AX.X, ALU.add).then_inc(setup_vec, 1)
            vec.tensor_reduce(group_of[:, :], ident[:, :].rearrange("p (g c) -> p g c", c=O),
                              AX.X, ALU.add).then_inc(setup_vec, 1)
            vec.tensor_reduce(pick_in_32[:, :], ident[:, :].rearrange("p (j c) -> p c j", c=32),
                              AX.X, ALU.add).then_inc(setup_vec, 1)
            vec.tensor_copy(spread16[:, :, :], ident[0:O, None, 0:O].to_broadcast([O, G8, O])).then_inc(setup_vec, 1)
            vec.tensor_copy(spread32[:, :, :], ident[0:O, None, 0:32].to_broadcast([O, 4, 32])).then_inc(setup_vec, 1)
            vec.wait_ge(setup_vec, 9)
            vec.tensor_copy(same_group[:, :, :],
                            group_of[:, :, None].to_broadcast([128, G8, O])).then_inc(setup_vec, 1)
            for l in range(2):
                vec.tensor_copy(place[:, l, O * (l + 1):O * (l + 2)], pick_in_group[:, :]).then_inc(setup_vec, 1)
            vec.wait_ge(setup_vec, 12)
            vec.nop().then_inc(const_vec, 1)
            nc_loop[0] = vec.Fori
            steps(step)


_TABLES = [f"tbl_{f}" for f in range(16)]
_INS = ["dense_ctx", "ids"] + _TABLES + ["W_top1", "b_top1", "W_top2", "b_top2", "W_top3", "L0_rec_Ws", "L0_rec_bs"]
_OUTS = [((1024, 1), "float32")]


def kernel(**inputs):
    import numpy as _np
    import concourse.bacc as _bacc
    from concourse import mybir as _mybir
    from concourse.bass_utils import run_bass_kernel_spmd as _run

    nc = _bacc.Bacc("TRN2", target_bir_lowering=False, num_devices=1)
    arrays, args = {}, {}
    for name in _INS:
        a = _np.ascontiguousarray(inputs[name])
        arrays[f"in_{name}"] = a
        args[name] = nc.dram_tensor(f"in_{name}", a.shape, _mybir.dt.from_np(a.dtype), kind="ExternalInput").ap()
    shape, dtype = _OUTS[0]
    y = nc.dram_tensor("out_y", shape, _mybir.dt.from_np(_np.dtype(dtype)), kind="ExternalOutput").ap()
    dlrm_tower(nc, args["dense_ctx"], args["ids"], [args[n] for n in _TABLES], args["W_top1"], args["b_top1"],
               args["W_top2"], args["b_top2"], args["W_top3"], args["L0_rec_Ws"], args["L0_rec_bs"], y)
    r = _run(nc, [arrays], core_ids=[0])
    return r.results[0]["out_y"]
```

```python
import concourse.bass as bass
from concourse import mybir
from contextlib import ExitStack


def dlrm_tower(nc, dense_ctx, ids, tables, W_top1, b_top1, W_top2, b_top2, W_top3, layer_W, layer_b, out):
    fp32 = mybir.dt.float32
    i32 = mybir.dt.int32
    ALU = mybir.AluOpType
    ACT = mybir.ActivationFunctionType
    AX = mybir.AxisListType

    B, F = ids.shape
    L, O, E = layer_W.shape
    T = B // 128
    H = E // 128
    HB = H * 128
    D = dense_ctx.shape[1]
    C1 = W_top1.shape[1] // 128
    C2 = W_top2.shape[1] // 128
    KIN = L * O + D
    G8 = 128 // O
    NP = F // 2

    POOL_ROWS = [(14, 15, 1), (13, 14, 2), (12, 13, 3), (8, 9, 7), (0, 1, 3), (0, 4, 12)]
    VEC_FIELDS = [11, 10, 9, 7, 6, 5, 4, 3, 2, 1]
    QUAD = 4
    RING_1 = 44
    RING = 48
    SPLIT = 80
    vec_segments = []
    at = 0
    for f in VEC_FIELDS:
        g, left = f + 1, F - 1 - f
        while left:
            n = min(left, RING_1 - at) if at < RING_1 else left
            if at < SPLIT < at + n:
                n = SPLIT - at
            vec_segments.append((f, g, n, at if at < RING_1 else at - RING_1, at))
            g, left, at = g + n, left - n, at + n
    VEC_PAIRS = at
    POOL_PAIRS = sum(n for _, _, n in POOL_ROWS)
    assert VEC_PAIRS + POOL_PAIRS == F * (F - 1) // 2 and VEC_PAIRS - RING_1 == RING
    NV = len(vec_segments)
    NPOOL = len(POOL_ROWS)
    VQ, PQ = VEC_PAIRS // QUAD, POOL_PAIRS // QUAD
    PROJ, V0, V1, V2, V3, DIAG, V4, P0, V5, P1 = range(10)
    USES = 10
    SETS = {DIAG: [("d", q) for q in range(4)], V0: [("v", q) for q in range(0, 4)],
            P0: [("p", q) for q in range(0, 4)], V1: [("v", q) for q in range(4, 8)],
            P1: [("p", q) for q in range(4, PQ)] + [("v", 20)], V2: [("v", q) for q in range(8, 12)],
            V3: [("v", q) for q in range(12, 16)], V4: [("v", q) for q in range(16, 20)],
            V5: [("v", q) for q in range(21, VQ)]}
    ORDER = sorted(SETS)
    NS = len(ORDER)
    RELUED = 8
    SQUARES = 4
    FPS = F // SQUARES
    OPERANDS = [5, 4, 3, 2, 1, 0]
    NOP = len(OPERANDS)

    def set_pairs(u):
        return QUAD * len(SETS[u]) // 4

    def last_segment(f_list):
        return max(i for i, s in enumerate(vec_segments) if s[0] in f_list)

    freed_after = [last_segment([f for f in VEC_FIELDS if f // 2 == n]) + 1 for n in OPERANDS]

    def segments_before_quad(q):
        need = QUAD * (q + 1)
        return min(i for i, s in enumerate(vec_segments) if s[4] + s[2] >= need) + 1

    def pool_rows_before_quad(q):
        total = 0
        for i, (_, _, n) in enumerate(POOL_ROWS):
            total += n
            if total >= QUAD * (q + 1):
                return i + 1

    def ring_guard(seg):
        _, _, n, slot, number = seg
        first_turn = number < RING_1
        readers = []
        for u, quads in SETS.items():
            for kind, q in quads:
                if kind != "v":
                    continue
                for s in range(QUAD * q, QUAD * q + QUAD):
                    turn1 = s < RING_1
                    if turn1 != first_turn and slot <= (s if turn1 else s - RING_1) < slot + n:
                        readers.append(u)
        return (1 if first_turn else 0), max(readers) if readers else None

    CH = 4
    OC = O // CH

    def count(per_tile, t, n):
        return per_tile * (t + 2) + n

    ctx = ExitStack()
    with ctx:
        def sb(name, shape, dt=fp32):
            return ctx.enter_context(nc.sbuf_tensor(name, shape, dt))

        def ps(name, shape):
            return ctx.enter_context(nc.psum_tensor(name, shape, fp32))

        def sem(name):
            return ctx.enter_context(nc.semaphore(name))

        ids_sb = sb("ids_sb", [128, 2, F], i32)
        X = [sb(f"X{p}", [128, F, E]) for p in range(2)]
        XT = [sb(f"XT{p}", [128, F, HB]) for p in range(2)]
        vec_pairs = sb("vec_pairs", [128, RING, HB])
        pool_pairs = sb("pool_pairs", [128, POOL_PAIRS, HB])
        squares = sb("squares", [128, F, HB])
        relued = sb("relued", [128, RELUED, 512])
        partial = sb("partial", [128, 4, 128])
        proj = sb("proj", [128, 4, 128])
        cross = sb("cross", [128, O, F * F])
        mlp_in = [sb(f"mlp_in{p}", [128, KIN]) for p in range(2)]
        mlp_inT = sb("mlp_inT", [KIN, 128])
        hidden1 = sb("hidden1", [128, C1, 128])
        hidden2 = sb("hidden2", [128, C2, 128])
        tick_word = sb("tick_word", [1, 1])
        y_row = sb("y_row", [1, 2, 128])
        ident = sb("ident", [128, 128])
        pick_in_32 = sb("pick_in_32", [128, 32])
        spread32 = sb("spread32", [O, 4, 32])
        layer_rows = sb("layer_rows", [L * O, E])
        bias_in = sb("bias_in", [O, 1])
        WT = sb("WT", [128, H, 64])
        bias0 = sb("bias0", [128, 2])
        bias12 = sb("bias12", [128, 2 * O])
        w1 = sb("w1", [KIN, C1, 128])
        w2 = sb("w2", [128, C1, C2 * 128])
        w3 = sb("w3", [128, C2])
        b1 = sb("b1", [128, C1])
        b2 = sb("b2", [128, C2])

        turn_bank = [ps(f"turn_bank{i}", [128, 512]) for i in range(2)]
        operand_bank = [ps(f"operand_bank{i}", [128, 512]) for i in range(2)]
        work_bank = [ps(f"work_bank{i}", [128, 512]) for i in range(2)]
        sum_bank = ps("sum_bank", [128, 512])
        proj_bank = ps("proj_bank", [128, 512])
        z0_ps = sum_bank[:, 0:O]
        mlp_inT_ps = turn_bank[1][0:KIN, 384:512]

        ids_in = [sem(f"ids_in{p}") for p in range(2)]
        dense_in = [sem(f"dense_in{p}") for p in range(2)]
        y_out = [sem(f"y_out{p}") for p in range(2)]
        gathered = [sem(f"gathered{f}") for f in range(F)]
        weights_in = sem("weights_in")
        mlp_weights_in = sem("mlp_weights_in")
        tick = sem("tick")
        const_pool = sem("const_pool")
        const_vec = sem("const_vec")
        setup_vec = sem("setup_vec")
        setup_pe = sem("setup_pe")
        setup_act = sem("setup_act")
        turned = sem("turned")
        xt_ready = sem("xt_ready")
        operand_ready = sem("operand_ready")
        vec_done = sem("vec_done")
        pool_done = sem("pool_done")
        squared = sem("squared")
        work_filled = sem("work_filled")
        work_drained = sem("work_drained")
        set_summed = sem("set_summed")
        sums_copied = sem("sums_copied")
        z0_ready = sem("z0_ready")
        z0_kept = sem("z0_kept")
        proj_ready = sem("proj_ready")
        crossed = sem("crossed")
        cross_summed = sem("cross_summed")
        mlp_pe = sem("mlp_pe")
        mlp_act = sem("mlp_act")
        MA = C1 + C2 + 2

        block = ctx.enter_context(nc.Block())

        def steps(step):
            step(0, 0, 0, True, True, False)
            with nc_loop[0](0, (T - 2) // 2) as i:
                step(2 * i + 1, 1, i, True, True, True)
                step(2 * i + 2, 0, i, True, True, True)
            step(T - 1, 1, (T - 2) // 2, True, False, True)
            step(T, 0, (T - 2) // 2, False, False, True)

        nc_loop = [None]

        @block.sync
        def _(sp):
            def fetch_ids(t, p, first):
                if not first:
                    sp.wait_ge(turned, NP * (t - 1))
                sp.dma_start(ids_sb[:, p, :], ids[bass.ds(t * 128, 128), :]).then_inc(ids_in[p], 16)

            def fetch_dense(t, p, first):
                if not first:
                    sp.wait_ge(mlp_pe, count(4, t - 2, 1))
                sp.dma_start(mlp_in[p][:, L * O:KIN],
                             dense_ctx[bass.ds(t * 128, 128), :]).then_inc(dense_in[p], 16)

            fetch_ids(0, 0, True)
            fetch_ids(1, 1, True)
            sp.dma_start(layer_rows[:, :], layer_W.rearrange("l o e -> (l o) e")).then_inc(weights_in, 16)
            sp.dma_start(bias12[:, :], layer_b.rearrange("l o -> (l o)")[None, O:L * O]
                         .to_broadcast([128, 2 * O])).then_inc(weights_in, 16)
            with nc.allow_non_contiguous_dma(reason="16 biases, once"):
                sp.dma_start(bias_in[:, :], layer_b[0:1, :].rearrange("l o -> o l")).then_inc(weights_in, 16)
            fetch_dense(0, 0, True)
            fetch_dense(1, 1, True)
            sp.dma_start(w1[:, :, :], W_top1.rearrange("k (c n) -> k c n", n=128)).then_inc(mlp_weights_in, 16)
            sp.dma_start(w2[:, :, :], W_top2.rearrange("(c k) n -> k c n", k=128)).then_inc(mlp_weights_in, 16)
            with nc.allow_non_contiguous_dma(reason="768 biases and 256 weights, once"):
                sp.dma_start(w3[:, :], W_top3.rearrange("(c k) o -> k (c o)", k=128)).then_inc(mlp_weights_in, 16)
                sp.dma_start(b1[:, :], b_top1.rearrange("(c k) -> k c", k=128)).then_inc(mlp_weights_in, 16)
                sp.dma_start(b2[:, :], b_top2.rearrange("(c k) -> k c", k=128)).then_inc(mlp_weights_in, 16)
            fetch_ids(2, 0, False)
            fetch_ids(3, 1, False)
            with sp.Fori(0, (T - 4) // 2) as i:
                fetch_dense(2 * i + 2, 0, False)
                fetch_ids(2 * i + 4, 0, False)
                fetch_dense(2 * i + 3, 1, False)
                fetch_ids(2 * i + 5, 1, False)
            fetch_dense(T - 2, 0, False)
            fetch_dense(T - 1, 1, False)

        @block.gpsimd
        def _(pool):
            def take_waits(n):
                if not (isinstance(n, int) and n == 0):
                    pool.wait_ge(tick, n)
                pool.tensor_tensor(tick_word[:, :], ident[0:1, 0:1], ident[0:1, 0:1], ALU.mult).then_inc(tick, 1)

            def gathers(t, p, k):
                first = isinstance(k, int) and k == 0
                pool.wait_ge(ids_in[p], 16 * (k + 1))
                if not first:
                    for f in range(F):
                        pool.wait_ge(gathered[f], 16 * t)
                    pool.wait_ge(turned, NP * (t - 1))
                    pool.wait_ge(operand_ready, NOP * (t - 2) + OPERANDS.index(4) + 1)
                    take_waits(3 * (t - 2) + 1)
                elif t == 1:
                    for f in range(F):
                        pool.wait_ge(gathered[f], 16)
                for f in reversed(range(F)):
                    if f == 7 and not first:
                        pool.wait_ge(operand_ready, NOP * (t - 2) + OPERANDS.index(1) + 1)
                        take_waits(3 * (t - 2) + 2)
                    if f == 1 and not first:
                        pool.wait_ge(operand_ready, NOP * (t - 1))
                        take_waits(3 * (t - 2) + 3)
                    pool.indirect_dma_start(
                        X[p][:, f, :], None, tables[f][:, :],
                        bass.IndirectOffsetOnAxis(ap=ids_sb[:, p, f:f + 1], axis=0)).then_inc(gathered[f], 16)

            def pairs(t, p):
                at = 0
                if not (isinstance(t, int) and t == 0):
                    pool.wait_ge(work_filled, USES * (t - 1) + P1 + 1)
                for f, g, n in POOL_ROWS:
                    pool.wait_ge(xt_ready, NP * t + NP - f // 2)
                    pool.tensor_tensor(pool_pairs[:, at:at + n, :],
                                       XT[p][:, f:f + 1, :].to_broadcast([128, n, HB]),
                                       XT[p][:, g:g + n, :], ALU.mult).then_inc(pool_done, 1)
                    at += n

            pool.memset(ident[:, :], 0.0).then_inc(const_pool, 1)
            pool.wait_ge(const_pool, 1)
            pool.affine_select(out=ident[:, :], in_=ident[:, :], compare_op=ALU.not_equal, fill=1.0,
                               base=0, pattern=[[-1, 128]], channel_multiplier=1).then_inc(const_pool, 1)
            gathers(0, 0, 0)
            gathers(1, 1, 0)
            pool.wait_ge(const_pool, 2)
            take_waits(0)
            pairs(0, 0)
            with pool.Fori(0, (T - 2) // 2) as i:
                gathers(2 * i + 2, 0, i + 1)
                pairs(2 * i + 1, 1)
                gathers(2 * i + 3, 1, i + 1)
                pairs(2 * i + 2, 0)
            pairs(T - 1, 1)

        @block.scalar
        def _(act):
            def turn_copy(t, p, n, first=False):
                m = NP - 1 - n
                act.wait_ge(turned, NP * t + m + 1)
                if m == 0 and not first:
                    act.wait_ge(vec_done, NV * (t - 1))
                    act.wait_ge(pool_done, NPOOL * (t - 1))
                    act.wait_ge(squared, SQUARES * (t - 1))
                    act.wait_ge(work_filled, USES * (t - 2) + PROJ + 1)
                act.activation(XT[p][:, 2 * n:2 * n + 2, :], turn_bank[m % 2][:, :], ACT.Copy).then_inc(xt_ready, 1)

            def square(t, p, i, first):
                if i == 0:
                    if not first:
                        act.wait_ge(work_filled, USES * (t - 1) + DIAG + 1)
                f = F - FPS * (i + 1)
                act.wait_ge(xt_ready, NP * t + NP - f // 2)
                act.activation(squares[:, f:f + FPS, :], XT[p][:, f:f + FPS, :], ACT.Square).then_inc(squared, 1)

            def relu_set(t, u, first):
                s = ORDER.index(u)
                act.wait_ge(work_filled, USES * t + u + 1)
                if s >= RELUED:
                    act.wait_ge(set_summed, NS * t + s - RELUED + 1)
                elif not first:
                    act.wait_ge(set_summed, NS * t)
                cols = 128 * set_pairs(u)
                twice = u != DIAG
                act.activation(relued[:, s % RELUED, 0:cols], work_bank[u % 2][:, 0:cols], ACT.Relu,
                               bias=bias0[:, 1:2] if twice else bias0[:, 0:1],
                               scale=2.0 if twice else 1.0).then_inc(work_drained, 1)

            def copy_sums(t):
                act.wait_ge(set_summed, NS * (t + 1))
                act.activation(partial[:, :, :], sum_bank[:, :], ACT.Copy).then_inc(sums_copied, 1)

            def copy_proj(t, first):
                act.wait_ge(work_filled, USES * t + PROJ + 1)
                if not first:
                    act.wait_ge(proj_ready, t)
                act.activation(proj[:, :, :], work_bank[PROJ % 2][:, :], ACT.Copy).then_inc(work_drained, 1)

            def sum_cross(t, p, l, c):
                act.wait_ge(crossed, count(2 * CH, t, CH * l + c + 1))
                for o in range(OC * c, OC * c + OC):
                    last = act.activation(cross[:, o, :], cross[:, o, :], ACT.Relu,
                                          bias=bias12[:, O * l + o:O * l + o + 1],
                                          accum_out=mlp_in[p][:, O * (l + 1) + o:O * (l + 1) + o + 1])
                last.then_inc(cross_summed, 1)

            def mlp(t, p, k, part):
                act.wait_ge(mlp_pe, count(4, t, part + 1))
                if part == 0:
                    act.activation(mlp_inT[:, :], mlp_inT_ps, ACT.Copy).then_inc(mlp_act, 1)
                elif part == 1:
                    for c in range(C1):
                        act.activation(hidden1[:, c, :], turn_bank[0][:, c * 128:(c + 1) * 128], ACT.Relu,
                                       bias=b1[:, c:c + 1]).then_inc(mlp_act, 1)
                elif part == 2:
                    for c in range(C2):
                        act.activation(hidden2[:, c, :], turn_bank[1][:, c * 128:(c + 1) * 128], ACT.Relu,
                                       bias=b2[:, c:c + 1]).then_inc(mlp_act, 1)
                else:
                    act.wait_ge(y_out[p], 16 * (k + 1))
                    act.activation(y_row[0:1, p, :], turn_bank[1][0:1, 256:384], ACT.Copy).then_inc(mlp_act, 1)
                    act.wait_ge(mlp_act, count(MA, t, MA))
                    act.dma_start(out[bass.ds(t * 128, 128), :].rearrange("b o -> o b"),
                                  y_row[0:1, p, :]).then_inc(y_out[p], 16)

            def step(t, p, k, front, fetch, back):
                first = isinstance(t, int) and t == 0
                q = 1 - p
                if front:
                    relu_set(t, V4, first)
                if fetch:
                    turn_copy(t + 1, q, 7, first)
                    turn_copy(t + 1, q, 6)
                    turn_copy(t + 1, q, 5)
                    square(t + 1, q, 0, False)
                    turn_copy(t + 1, q, 4)
                    turn_copy(t + 1, q, 3)
                if back:
                    sum_cross(t - 1, q, 1, 1)
                if fetch:
                    turn_copy(t + 1, q, 2)
                    square(t + 1, q, 1, False)
                    turn_copy(t + 1, q, 1)
                if front:
                    relu_set(t, P0, first)
                if fetch:
                    square(t + 1, q, 2, False)
                if front:
                    relu_set(t, V5, first)
                if back:
                    sum_cross(t - 1, q, 1, 2)
                if fetch:
                    turn_copy(t + 1, q, 0)
                if front:
                    relu_set(t, P1, first)
                    copy_sums(t)
                if fetch:
                    square(t + 1, q, 3, False)
                if back:
                    sum_cross(t - 1, q, 1, 3)
                if front:
                    sum_cross(t, p, 0, 0)
                if back:
                    mlp(t - 1, q, k, 0)
                if fetch:
                    copy_proj(t + 1, False)
                    relu_set(t + 1, V0, False)
                if front:
                    sum_cross(t, p, 0, 1)
                if back:
                    mlp(t - 1, q, k, 1)
                if front:
                    sum_cross(t, p, 0, 2)
                if fetch:
                    relu_set(t + 1, V1, False)
                if front:
                    sum_cross(t, p, 0, 3)
                if back:
                    mlp(t - 1, q, k, 2)
                if fetch:
                    relu_set(t + 1, V2, False)
                    relu_set(t + 1, V3, False)
                if front:
                    sum_cross(t, p, 1, 0)
                if back:
                    mlp(t - 1, q, k, 3)
                if fetch:
                    relu_set(t + 1, DIAG, False)

            act.wait_ge(setup_pe, 1)
            act.wait_ge(const_vec, 1)
            for h in range(H):
                act.activation(WT[:, h, 0:O], work_bank[0][:, 48 * h:48 * h + O], ACT.Copy).then_inc(setup_act, 1)
                act.activation(WT[:, h, 2 * O:4 * O], work_bank[0][:, 48 * h + O:48 * h + 3 * O],
                               ACT.Copy).then_inc(setup_act, 1)
            for i in range(2):
                act.activation(bias0[:, i:i + 1], work_bank[0][:, 128:129], ACT.Copy,
                               scale=1.0 + i).then_inc(setup_act, 1)
            act.wait_ge(setup_act, 6)
            act.nop().then_inc(cross_summed, 2 * 2 * CH)
            act.nop().then_inc(mlp_act, 2 * MA)
            for p in range(2):
                act.nop().then_inc(y_out[p], 16)
            turn_copy(0, 0, 7, True)
            turn_copy(0, 0, 6, True)
            turn_copy(0, 0, 5, True)
            square(0, 0, 0, True)
            turn_copy(0, 0, 4, True)
            turn_copy(0, 0, 3, True)
            turn_copy(0, 0, 2, True)
            square(0, 0, 1, True)
            turn_copy(0, 0, 1, True)
            square(0, 0, 2, True)
            turn_copy(0, 0, 0, True)
            square(0, 0, 3, True)
            copy_proj(0, True)
            relu_set(0, V0, True)
            relu_set(0, V1, True)
            relu_set(0, V2, True)
            relu_set(0, V3, True)
            relu_set(0, DIAG, True)
            act.wait_ge(mlp_weights_in, 80)
            nc_loop[0] = act.Fori
            steps(step)
            for p in range(2):
                act.wait_ge(y_out[p], 16 * (T // 2 + 1))

        @block.tensor
        def _(pe):
            def turn(t, p, n, first=False):
                m = NP - 1 - n
                for f in (2 * n + 1, 2 * n):
                    pe.wait_ge(gathered[f], 16 * (t + 1))
                if not (first and m < 2):
                    pe.wait_ge(xt_ready, NP * t + m - 1)
                if m < 2 and not first:
                    pe.wait_ge(mlp_act, count(MA, t - 3, 1 + C1 if m == 0 else MA))
                for i in range(2):
                    for h in range(H):
                        last = pe.transpose(turn_bank[m % 2][:, 256 * i + 128 * h:256 * i + 128 * h + 128],
                                            X[p][:, 2 * n + i, 128 * h:128 * h + 128], ident[:, :])
                last.then_inc(turned, 1)

            def operand(t, p, m, first=False):
                n = OPERANDS[m]
                if m >= 2:
                    pe.wait_ge(vec_done, NV * t + freed_after[m - 2])
                elif not first:
                    pe.wait_ge(vec_done, NV * (t - 1) + freed_after[NOP - 2 + m])
                for f in (2 * n, 2 * n + 1):
                    pe.wait_ge(gathered[f], 16 * (t + 1))
                for i in range(2):
                    for h in range(H):
                        last = pe.transpose(
                            operand_bank[m % 2][:, 256 * i + 128 * h:256 * i + 128 * h + 128],
                            X[p][:, 2 * n + i, 128 * h:128 * h + 128], ident[:, :])
                last.then_inc(operand_ready, 1)

            def wait_work_bank(t, u, first):
                if not (first and u < 2):
                    pe.wait_ge(work_drained, USES * t + u - 1)

            def contract(t, u, first):
                wait_work_bank(t, u, first)
                for kind in ("v", "p", "d"):
                    quads = [q for k, q in SETS[u] if k == kind]
                    if quads and kind == "v":
                        pe.wait_ge(vec_done, NV * t + segments_before_quad(quads[-1]))
                    elif quads and kind == "p":
                        pe.wait_ge(pool_done, NPOOL * t + pool_rows_before_quad(quads[-1]))
                    elif quads:
                        pe.wait_ge(squared, SQUARES * (t + 1))
                for h in range(H):
                    n = set_pairs(u)
                    for j in range(4):
                        kind, q = SETS[u][n * j // QUAD]
                        slot = QUAD * q + n * j % QUAD
                        if kind == "v" and slot >= RING_1:
                            slot -= RING_1
                        src = {"v": vec_pairs, "p": pool_pairs, "d": squares}[kind]
                        last = pe.matmul(work_bank[u % 2][32 * j:32 * j + 32, 0:128 * n], WT[:, h, 0:32],
                                         src[:, slot:slot + n, 128 * h:128 * h + 128],
                                         start=(h == 0), stop=(h == H - 1))
                last.then_inc(work_filled, 1)

            def add_sets(t, n, first):
                uses = ORDER[4 * n:4 * n + 4]
                pe.wait_ge(work_drained, USES * t + uses[-1] + 1)
                if n == 0 and not first:
                    pe.wait_ge(z0_kept, count(1, t - 1, 1))
                for u in uses:
                    s = ORDER.index(u)
                    j = s % 4
                    cols = 128 * set_pairs(u)
                    pe.matmul(sum_bank[32 * j:32 * j + 32, 0:cols], pick_in_32[:, :], relued[:, s % RELUED, 0:cols],
                              start=(s < 4), stop=(s + 4 >= NS)).then_inc(set_summed, 1)

            def project(t, p, first):
                wait_work_bank(t, PROJ, first)
                pe.wait_ge(xt_ready, NP * (t + 1))
                for h in range(H):
                    for j in range(4):
                        last = pe.matmul(work_bank[PROJ % 2][32 * j:32 * j + 32, :], WT[:, h, 32:64],
                                         XT[p][:, 4 * j:4 * j + 4, 128 * h:128 * h + 128],
                                         start=(h == 0), stop=(h == H - 1))
                last.then_inc(work_filled, 1)

            def turn_proj(t):
                pe.wait_ge(work_drained, USES * t + PROJ + 1)
                pe.wait_ge(crossed, count(2 * CH, t - 1, 2 * CH))
                for i in range(4):
                    last = pe.transpose(proj_bank[:, 128 * i:128 * i + 128], proj[:, i, :], ident[:, :])
                last.then_inc(proj_ready, 1)

            def finish_z0(t):
                pe.wait_ge(sums_copied, t + 1)
                pe.wait_ge(z0_kept, count(1, t - 1, 1))
                for k in range(4):
                    last = pe.matmul(z0_ps, partial[:, k, :], pick_in_32[:, 0:O], start=(k == 0), stop=(k == 3))
                last.then_inc(z0_ready, 1)

            def last_tile(t):
                return isinstance(t, int) and t == T - 1

            def near_end(t):
                return isinstance(t, int) and t >= T - 2

            def mlp(t, p, k, part):
                if part == 0:
                    pe.wait_ge(cross_summed, count(2 * CH, t, 2 * CH))
                    pe.wait_ge(z0_kept, count(1, t, 1))
                    pe.wait_ge(xt_ready, NP * T if near_end(t) else NP * (t + 3))
                    if last_tile(t):
                        pe.wait_ge(mlp_act, count(MA, t - 1, MA))
                    pe.wait_ge(dense_in[p], 16 * (k + 1))
                    pe.matmul(mlp_inT_ps, mlp_in[p][:, :], ident[:, :], start=True, stop=True).then_inc(mlp_pe, 1)
                elif part == 1:
                    pe.wait_ge(mlp_act, count(MA, t, 1))
                    for c in range(C1):
                        last = pe.matmul(turn_bank[0][:, c * 128:(c + 1) * 128], w1[:, c, :], mlp_inT[:, :],
                                         start=True, stop=True)
                    last.then_inc(mlp_pe, 1)
                elif part == 2:
                    pe.wait_ge(mlp_act, count(MA, t, 1 + C1))
                    for m in range(C2):
                        for c in range(C1):
                            last = pe.matmul(turn_bank[1][:, m * 128:(m + 1) * 128], w2[:, c, m * 128:(m + 1) * 128],
                                             hidden1[:, c, :], start=(c == 0), stop=(c == C1 - 1))
                    last.then_inc(mlp_pe, 1)
                else:
                    pe.wait_ge(mlp_act, count(MA, t, 1 + C1 + C2))
                    for m in range(C2):
                        last = pe.matmul(turn_bank[1][0:1, 256:384], w3[:, m:m + 1], hidden2[:, m, :],
                                         start=(m == 0), stop=(m == C2 - 1))
                    last.then_inc(mlp_pe, 1)

            def step(t, p, k, front, fetch, back):
                first = isinstance(t, int) and t == 0
                q = 1 - p
                if fetch:
                    turn(t + 1, q, 7)
                if front:
                    add_sets(t, 0, first)
                    contract(t, V4, first)
                if fetch:
                    turn(t + 1, q, 6)
                    turn(t + 1, q, 5)
                    operand(t + 1, q, 0)
                    turn(t + 1, q, 4)
                    operand(t + 1, q, 1)
                    turn(t + 1, q, 3)
                if front:
                    contract(t, P0, first)
                if fetch:
                    turn(t + 1, q, 2)
                    operand(t + 1, q, 2)
                    turn(t + 1, q, 1)
                    operand(t + 1, q, 3)
                    turn(t + 1, q, 0)
                if front:
                    contract(t, V5, first)
                    contract(t, P1, first)
                    add_sets(t, 1, first)
                    add_sets(t, 2, first)
                    turn_proj(t)
                    finish_z0(t)
                if fetch:
                    operand(t + 1, q, 4)
                    project(t + 1, q, False)
                    contract(t + 1, V0, False)
                if back:
                    mlp(t - 1, q, k, 0)
                    mlp(t - 1, q, k, 1)
                if fetch:
                    contract(t + 1, V1, False)
                    contract(t + 1, V2, False)
                if back:
                    mlp(t - 1, q, k, 2)
                if fetch:
                    operand(t + 1, q, 5)
                    contract(t + 1, V3, False)
                if back:
                    mlp(t - 1, q, k, 3)
                if fetch:
                    contract(t + 1, DIAG, False)

            pe.wait_ge(const_pool, 2)
            pe.wait_ge(const_vec, 1)
            pe.wait_ge(weights_in, 48)
            for h in range(H):
                pe.transpose(work_bank[0][:, 48 * h:48 * h + 48], layer_rows[:, 128 * h:128 * h + 128],
                             ident[0:L * O, 0:L * O])
            pe.matmul(work_bank[0][:, 128:129], spread32[:, :, :], bias_in[:, :], start=True,
                      stop=True).then_inc(setup_pe, 1)
            pe.nop().then_inc(mlp_pe, 2 * 4)
            pe.wait_ge(setup_act, 6)
            turn(0, 0, 7, True)
            turn(0, 0, 6, True)
            turn(0, 0, 5, True)
            operand(0, 0, 0, True)
            turn(0, 0, 4, True)
            operand(0, 0, 1, True)
            turn(0, 0, 3, True)
            turn(0, 0, 2, True)
            operand(0, 0, 2, True)
            turn(0, 0, 1, True)
            operand(0, 0, 3, True)
            turn(0, 0, 0, True)
            operand(0, 0, 4, True)
            project(0, 0, True)
            contract(0, V0, True)
            contract(0, V1, True)
            contract(0, V2, True)
            operand(0, 0, 5, True)
            contract(0, V3, True)
            contract(0, DIAG, True)
            pe.wait_ge(mlp_weights_in, 80)
            nc_loop[0] = pe.Fori
            steps(step)

        @block.vector
        def _(vec):
            def segments(t, p, begin, end, first):
                for seg in vec_segments[begin:end + 1]:
                    f, g, n, slot, _ = seg
                    m = OPERANDS.index(f // 2)
                    vec.wait_ge(operand_ready, NOP * t + m + 1)
                    vec.wait_ge(xt_ready, NP * t + NP - (g // 2))
                    back, use = ring_guard(seg)
                    if use is not None and not (first and back):
                        vec.wait_ge(work_filled, USES * (t - back) + use + 1)
                    col = 256 * (f % 2)
                    vec.tensor_tensor(vec_pairs[:, slot:slot + n, :],
                                      operand_bank[m % 2][:, None, col:col + HB].to_broadcast([128, n, HB]),
                                      XT[p][:, g:g + n, :], ALU.mult).then_inc(vec_done, 1)

            def keep_z0(t, p):
                vec.wait_ge(z0_ready, t + 1)
                vec.wait_ge(mlp_pe, count(4, t - 2, 1))
                vec.tensor_copy(mlp_in[p][:, 0:O], z0_ps).then_inc(z0_kept, 1)

            def cross_products(t, p, l, c):
                if l == 0:
                    vec.wait_ge(z0_kept, count(1, t, 1))
                    vec.wait_ge(proj_ready, t + 1)
                    vec.wait_ge(cross_summed, count(2 * CH, t - 1, CH + c + 1))
                else:
                    vec.wait_ge(cross_summed, count(2 * CH, t, CH))
                z = mlp_in[p][:, None, O * l:O * l + O, None].to_broadcast([128, OC, O, F])
                P = proj_bank[:, :].rearrange("p (x l o) -> p l o x", l=2, o=O)
                vec.tensor_tensor(cross[:, OC * c:OC * c + OC, :].rearrange("p o (g x) -> p o g x", x=F),
                                  z, P[:, l, OC * c:OC * c + OC, None, :].to_broadcast([128, OC, O, F]),
                                  ALU.mult).then_inc(crossed, 1)

            def step(t, p, k, front, fetch, back):
                first = isinstance(t, int) and t == 0
                q = 1 - p
                if front:
                    segments(t, p, 0, 5, first)
                if back:
                    keep_z0(t - 1, q)
                if front:
                    segments(t, p, 6, 6, first)
                if back:
                    cross_products(t - 1, q, 0, 0)
                    cross_products(t - 1, q, 0, 1)
                    cross_products(t - 1, q, 0, 2)
                if front:
                    segments(t, p, 7, 7, first)
                if back:
                    cross_products(t - 1, q, 0, 3)
                if front:
                    segments(t, p, 8, 9, first)
                if back:
                    cross_products(t - 1, q, 1, 0)
                if front:
                    segments(t, p, 10, 10, first)
                if back:
                    cross_products(t - 1, q, 1, 1)
                if front:
                    segments(t, p, 11, 11, first)
                if back:
                    cross_products(t - 1, q, 1, 2)
                    cross_products(t - 1, q, 1, 3)

            vec.memset(WT[:, :, :], 0.0).then_inc(setup_vec, 1)
            vec.wait_ge(const_pool, 2)
            vec.tensor_reduce(pick_in_32[:, :], ident[:, :].rearrange("p (j c) -> p c j", c=32),
                              AX.X, ALU.add).then_inc(setup_vec, 1)
            vec.tensor_copy(spread32[:, :, :], ident[0:O, None, 0:32].to_broadcast([O, 4, 32])).then_inc(setup_vec, 1)
            vec.wait_ge(setup_vec, 3)
            vec.nop().then_inc(const_vec, 1)
            vec.nop().then_inc(z0_kept, 2)
            vec.nop().then_inc(crossed, 2 * 2 * CH)
            nc_loop[0] = vec.Fori
            steps(step)


_TABLES = [f"tbl_{f}" for f in range(16)]
_INS = ["dense_ctx", "ids"] + _TABLES + ["W_top1", "b_top1", "W_top2", "b_top2", "W_top3", "L0_rec_Ws", "L0_rec_bs"]
_OUTS = [((1024, 1), "float32")]


def kernel(**inputs):
    import numpy as _np
    import concourse.bacc as _bacc
    from concourse import mybir as _mybir
    from concourse.bass_utils import run_bass_kernel_spmd as _run

    nc = _bacc.Bacc("TRN2", target_bir_lowering=False, num_devices=1)
    arrays, args = {}, {}
    for name in _INS:
        a = _np.ascontiguousarray(inputs[name])
        arrays[f"in_{name}"] = a
        args[name] = nc.dram_tensor(f"in_{name}", a.shape, _mybir.dt.from_np(a.dtype), kind="ExternalInput").ap()
    shape, dtype = _OUTS[0]
    y = nc.dram_tensor("out_y", shape, _mybir.dt.from_np(_np.dtype(dtype)), kind="ExternalOutput").ap()
    dlrm_tower(nc, args["dense_ctx"], args["ids"], [args[n] for n in _TABLES], args["W_top1"], args["b_top1"],
               args["W_top2"], args["b_top2"], args["W_top3"], args["L0_rec_Ws"], args["L0_rec_bs"], y)
    r = _run(nc, [arrays], core_ids=[0])
    return r.results[0]["out_y"]
```

```python
import concourse.bass as bass
from concourse import mybir
from contextlib import ExitStack


def dlrm_tower(nc, dense_ctx, ids, tables, W_top1, b_top1, W_top2, b_top2, W_top3, layer_W, layer_b, out):
    fp32 = mybir.dt.float32
    i32 = mybir.dt.int32
    ALU = mybir.AluOpType
    ACT = mybir.ActivationFunctionType
    AX = mybir.AxisListType

    B, F = ids.shape
    L, O, E = layer_W.shape
    T = B // 128
    H = E // 128
    HB = H * 128
    D = dense_ctx.shape[1]
    C1 = W_top1.shape[1] // 128
    C2 = W_top2.shape[1] // 128
    KIN = L * O + D
    NP = F // 2
    BANK = 512

    POOL_ROWS = [(14, 15, 1), (13, 14, 2), (12, 13, 3), (6, 7, 9), (0, 1, 3), (0, 4, 12)]
    VEC_FIELDS = [11, 10, 9, 8, 7, 5, 4, 3, 2, 1]
    RING_1 = 44
    RING = 46
    SPLIT = 80
    vec_segments = []
    at = 0
    for f in VEC_FIELDS:
        g, left = f + 1, F - 1 - f
        while left:
            n = min(left, RING_1 - at) if at < RING_1 else left
            if at < SPLIT < at + n:
                n = SPLIT - at
            vec_segments.append((f, g, n, at if at < RING_1 else at - RING_1, at))
            g, left, at = g + n, left - n, at + n
    VEC_PAIRS = at
    POOL_PAIRS = sum(n for _, _, n in POOL_ROWS)
    assert VEC_PAIRS + POOL_PAIRS == F * (F - 1) // 2 and VEC_PAIRS - RING_1 == RING
    NV = len(vec_segments)
    NPOOL = len(POOL_ROWS)
    V0, V1, PROJ, V2, V3, DIAG, P0, V4, P1, V5 = range(10)
    USES = 10
    SETS = {V0: (4, [("v", 0), ("v", 4), ("v", 8), ("v", 12)]),
            V1: (4, [("v", 16), ("v", 20), ("v", 24), ("v", 28)]),
            V2: (4, [("v", 32), ("v", 36), ("v", 40), ("v", 44)]),
            V3: (4, [("v", 48), ("v", 52), ("v", 56), ("v", 60)]),
            V4: (4, [("v", 64), ("v", 68), ("v", 72), ("v", 76)]),
            V5: (2, [("v", 84), ("v", 86), ("v", 88), ("p", 28)]),
            P0: (4, [("p", 0), ("p", 4), ("p", 8), ("p", 12)]),
            P1: (4, [("p", 16), ("p", 20), ("p", 24), ("v", 80)]),
            DIAG: (4, [("d", 0), ("d", 4), ("d", 8), ("d", 12)])}
    assert sum(4 * n for n, _ in SETS.values()) == VEC_PAIRS + POOL_PAIRS + F
    ORDER = sorted(SETS)
    NS = len(ORDER)
    RELUED = 8
    SQUARES = 4
    FPS = F // SQUARES
    OPERANDS = [5, 4, 3, 2, 1, 0]
    NOP = len(OPERANDS)

    EARLY = NPOOL - 1
    LATE = NV - 1

    def last_segment(f_list):
        return max(i for i, s in enumerate(vec_segments) if s[0] in f_list)

    freed_after = [last_segment([f for f in VEC_FIELDS if f // 2 == n]) + 1 for n in OPERANDS]

    def segments_before(pairs):
        return min(i for i, s in enumerate(vec_segments) if s[4] + s[2] >= pairs) + 1

    def pool_rows_before(pairs):
        total = 0
        for i, (_, _, n) in enumerate(POOL_ROWS):
            total += n
            if total >= pairs:
                return i + 1

    def last_reader(buffer, begin, n):
        return max(u for u, (per_group, groups) in SETS.items() for kind, first in groups
                   if kind == buffer and first < begin + n and begin < first + per_group)

    def ring_guard(seg):
        _, _, n, slot, number = seg
        first_turn = number < RING_1
        readers = []
        for u, (per_group, groups) in SETS.items():
            for kind, begin in groups:
                for s in range(begin, begin + per_group):
                    turn1 = s < RING_1
                    if kind == "v" and turn1 != first_turn and slot <= (s if turn1 else s - RING_1) < slot + n:
                        readers.append(u)
        return (1 if first_turn else 0), max(readers) if readers else None

    CH = 4
    OC = O // CH

    def count(per_tile, t, n):
        return per_tile * (t + 2) + n

    ctx = ExitStack()
    with ctx:
        def sb(name, shape, dt=fp32):
            return ctx.enter_context(nc.sbuf_tensor(name, shape, dt))

        def ps(name, shape):
            return ctx.enter_context(nc.psum_tensor(name, shape, fp32))

        def sem(name):
            return ctx.enter_context(nc.semaphore(name))

        ids_sb = sb("ids_sb", [128, 2, F], i32)
        X = [sb(f"X{p}", [128, F, E]) for p in range(2)]
        XT = [sb(f"XT{p}", [128, F, HB]) for p in range(2)]
        vec_pairs = sb("vec_pairs", [128, RING, HB])
        pool_pairs = sb("pool_pairs", [128, POOL_PAIRS, HB])
        squares = sb("squares", [128, F, HB])
        relued = sb("relued", [128, RELUED, BANK])
        partial = sb("partial", [128, 4, 128])
        proj = sb("proj", [128, 4, 128])
        cross = sb("cross", [128, O, F * F])
        mlp_in = [sb(f"mlp_in{p}", [128, KIN]) for p in range(2)]
        mlp_inT = sb("mlp_inT", [KIN, 128])
        hidden1 = sb("hidden1", [128, C1, 128])
        hidden2 = sb("hidden2", [128, C2, 128])
        tick_word = sb("tick_word", [1, 1])
        done_word = sb("done_word", [1, 1])
        y_row = sb("y_row", [1, 2, 128])
        ident = sb("ident", [128, 128])
        pick_in_32 = sb("pick_in_32", [128, 32])
        spread32 = sb("spread32", [O, 4, 32])
        layer_rows = sb("layer_rows", [L * O, E])
        bias_in = sb("bias_in", [O, 1])
        WT = sb("WT", [128, H, 64])
        bias0 = sb("bias0", [128, 2])
        bias12 = sb("bias12", [128, 2 * O])
        w1 = sb("w1", [KIN, C1, 128])
        w2 = sb("w2", [128, C1, C2 * 128])
        w3 = sb("w3", [128, C2])
        b1 = sb("b1", [128, C1])
        b2 = sb("b2", [128, C2])

        turn_bank = [ps(f"turn_bank{i}", [128, BANK]) for i in range(2)]
        operand_bank = [ps(f"operand_bank{i}", [128, BANK]) for i in range(2)]
        work_bank = [ps(f"work_bank{i}", [128, BANK]) for i in range(2)]
        sum_bank = ps("sum_bank", [128, BANK])
        proj_bank = ps("proj_bank", [128, BANK])
        z0_ps = sum_bank[:, 0:O]
        mlp_inT_ps = turn_bank[1][0:KIN, 3 * 128:BANK]
        y_ps = turn_bank[1][0:1, C2 * 128:C2 * 128 + 128]

        ids_in = [sem(f"ids_in{p}") for p in range(2)]
        dense_in = [sem(f"dense_in{p}") for p in range(2)]
        y_out = [sem(f"y_out{p}") for p in range(2)]
        gathered = [sem(f"gathered{f}") for f in range(F)]
        weights_in = sem("weights_in")
        mlp_weights_in = sem("mlp_weights_in")
        tick = sem("tick")
        const_pool = sem("const_pool")
        const_vec = sem("const_vec")
        setup_vec = sem("setup_vec")
        setup_pe = sem("setup_pe")
        setup_act = sem("setup_act")
        turned = sem("turned")
        xt_ready = sem("xt_ready")
        operand_ready = sem("operand_ready")
        vec_done = sem("vec_done")
        pool_done = sem("pool_done")
        early_done = sem("early_done")
        squared = sem("squared")
        work_filled = sem("work_filled")
        work_drained = sem("work_drained")
        set_summed = sem("set_summed")
        sums_copied = sem("sums_copied")
        z0_ready = sem("z0_ready")
        z0_kept = sem("z0_kept")
        proj_ready = sem("proj_ready")
        crossed = sem("crossed")
        cross_summed = sem("cross_summed")
        mlp_pe = sem("mlp_pe")
        mlp_act = sem("mlp_act")
        MP = 4
        MA = C1 + C2 + 2

        block = ctx.enter_context(nc.Block())

        zero = WT[:, 0, O:O + 1]
        CUT = 10

        def cross_of(t):
            return X[T % 2] if is_tile(t, T - 1) else cross

        def is_tile(t, *numbers):
            return isinstance(t, int) and t in numbers

        @block.sync
        def _(sp):
            def fetch_ids(t, p, first):
                if not first:
                    sp.wait_ge(turned, NP * (t - 1))
                sp.dma_start(ids_sb[:, p, :], ids[bass.ds(t * 128, 128), :]).then_inc(ids_in[p], 16)

            def fetch_dense(t, p, first):
                if not first:
                    sp.wait_ge(mlp_pe, count(MP, t - 2, 1))
                sp.dma_start(mlp_in[p][:, L * O:KIN],
                             dense_ctx[bass.ds(t * 128, 128), :]).then_inc(dense_in[p], 16)

            fetch_ids(0, 0, True)
            fetch_ids(1, 1, True)
            sp.dma_start(layer_rows[:, :], layer_W.rearrange("l o e -> (l o) e")).then_inc(weights_in, 16)
            sp.dma_start(bias12[:, :], layer_b.rearrange("l o -> (l o)")[None, O:L * O]
                         .to_broadcast([128, 2 * O])).then_inc(weights_in, 16)
            with nc.allow_non_contiguous_dma(reason="16 biases, once"):
                sp.dma_start(bias_in[:, :], layer_b[0:1, :].rearrange("l o -> o l")).then_inc(weights_in, 16)
            fetch_dense(0, 0, True)
            fetch_dense(1, 1, True)
            sp.dma_start(w1[:, :, :], W_top1.rearrange("k (c n) -> k c n", n=128)).then_inc(mlp_weights_in, 16)
            sp.dma_start(w2[:, :, :], W_top2.rearrange("(c k) n -> k c n", k=128)).then_inc(mlp_weights_in, 16)
            with nc.allow_non_contiguous_dma(reason="768 biases and 256 weights, once"):
                sp.dma_start(w3[:, :], W_top3.rearrange("(c k) o -> k (c o)", k=128)).then_inc(mlp_weights_in, 16)
                sp.dma_start(b1[:, :], b_top1.rearrange("(c k) -> k c", k=128)).then_inc(mlp_weights_in, 16)
                sp.dma_start(b2[:, :], b_top2.rearrange("(c k) -> k c", k=128)).then_inc(mlp_weights_in, 16)
            fetch_ids(2, 0, False)
            fetch_ids(3, 1, False)
            with sp.Fori(0, (T - 4) // 2) as i:
                fetch_dense(2 * i + 2, 0, False)
                fetch_ids(2 * i + 4, 0, False)
                fetch_dense(2 * i + 3, 1, False)
                fetch_ids(2 * i + 5, 1, False)
            fetch_dense(T - 2, 0, False)
            fetch_dense(T - 1, 1, False)

        @block.gpsimd
        def _(pool):
            def take_waits(n):
                if not (isinstance(n, int) and n == 0):
                    pool.wait_ge(tick, n)
                pool.tensor_tensor(tick_word[:, :], ident[0:1, 0:1], ident[0:1, 0:1], ALU.mult).then_inc(tick, 1)

            def gathers(t, p, k):
                first = isinstance(k, int) and k == 0
                pool.wait_ge(ids_in[p], 16 * (k + 1))
                if not first:
                    for f in range(F):
                        pool.wait_ge(gathered[f], 16 * t)
                    pool.wait_ge(turned, NP * (t - 1))
                    pool.wait_ge(operand_ready, NOP * (t - 2) + OPERANDS.index(4) + 1)
                    take_waits(3 * (t - 2) + 1)
                for f in reversed(range(F)):
                    if is_tile(t, 1):
                        pool.wait_ge(gathered[f], 16)
                    if f == 7 and not first:
                        pool.wait_ge(operand_ready, NOP * (t - 2) + OPERANDS.index(1) + 1)
                        take_waits(3 * (t - 2) + 2)
                    if f == 1 and not first:
                        pool.wait_ge(operand_ready, NOP * (t - 1))
                        take_waits(3 * (t - 2) + 3)
                    pool.indirect_dma_start(
                        X[p][:, f, :], None, tables[f][:, :],
                        bass.IndirectOffsetOnAxis(ap=ids_sb[:, p, f:f + 1], axis=0)).then_inc(gathered[f], 16)

            def pairs(t, p):
                at = 0
                for i, (f, g, n) in enumerate(POOL_ROWS):
                    if is_tile(t, 0) and i == EARLY:
                        pool.wait_ge(early_done, 1)
                        pool.tensor_tensor(done_word[:, :], ident[0:1, 0:1], ident[0:1, 0:1],
                                           ALU.mult).then_inc(pool_done, 1)
                        continue
                    if not is_tile(t, 0):
                        pool.wait_ge(work_filled, USES * (t - 1) + last_reader("p", at, n) + 1)
                    pool.wait_ge(xt_ready, NP * t + NP - f // 2)
                    pool.tensor_tensor(pool_pairs[:, at:at + n, :],
                                       XT[p][:, f:f + 1, :].to_broadcast([128, n, HB]),
                                       XT[p][:, g:g + n, :], ALU.mult).then_inc(pool_done, 1)
                    at += n

            def late_segment(t, p):
                f, g, n, slot, _ = vec_segments[LATE]
                pool.wait_ge(xt_ready, NP * (t + 1))
                pool.wait_ge(work_filled, USES * t + ring_guard(vec_segments[LATE])[1] + 1)
                pool.tensor_tensor(vec_pairs[:, slot:slot + n, :], XT[p][:, f:f + 1, :].to_broadcast([128, n, HB]),
                                   XT[p][:, g:g + n, :], ALU.mult).then_inc(pool_done, 1)

            pool.memset(ident[:, :], 0.0).then_inc(const_pool, 1)
            pool.wait_ge(const_pool, 1)
            pool.affine_select(out=ident[:, :], in_=ident[:, :], compare_op=ALU.not_equal, fill=1.0,
                               base=0, pattern=[[-1, 128]], channel_multiplier=1).then_inc(const_pool, 1)
            gathers(0, 0, 0)
            gathers(1, 1, 0)
            pool.wait_ge(const_pool, 2)
            take_waits(0)
            pairs(0, 0)
            with pool.Fori(0, (T - 2) // 2) as i:
                gathers(2 * i + 2, 0, i + 1)
                pairs(2 * i + 1, 1)
                gathers(2 * i + 3, 1, i + 1)
                pairs(2 * i + 2, 0)
            pairs(T - 1, 1)
            late_segment(T - 1, 1)

        @block.scalar
        def _(act):
            def turn_copy(t, p, n):
                m = NP - 1 - n
                act.wait_ge(turned, NP * t + m + 1)
                if m == 0 and not is_tile(t, 0, 1):
                    act.wait_ge(vec_done, NV * (t - 1))
                    act.wait_ge(pool_done, NPOOL * (t - 1))
                    act.wait_ge(squared, SQUARES * (t - 1))
                    act.wait_ge(work_filled, USES * (t - 2) + PROJ + 1)
                act.activation(XT[p][:, 2 * n:2 * n + 2, :], turn_bank[m % 2][:, :], ACT.Copy).then_inc(xt_ready, 1)

            def square(t, p, i):
                if i == 0 and not is_tile(t, 0):
                    act.wait_ge(work_filled, USES * (t - 1) + DIAG + 1)
                f = F - FPS * (i + 1)
                act.wait_ge(xt_ready, NP * t + NP - f // 2)
                act.activation(squares[:, f:f + FPS, :], XT[p][:, f:f + FPS, :], ACT.Square).then_inc(squared, 1)

            def relu_set(t, u):
                s = ORDER.index(u)
                act.wait_ge(work_filled, USES * t + u + 1)
                if s >= RELUED:
                    act.wait_ge(set_summed, NS * t + s - RELUED + 1)
                elif not is_tile(t, 0):
                    act.wait_ge(set_summed, NS * t)
                cols = 128 * SETS[u][0]
                twice = u != DIAG
                act.activation(relued[:, s % RELUED, 0:cols], work_bank[u % 2][:, 0:cols], ACT.Relu,
                               bias=bias0[:, 1:2] if twice else bias0[:, 0:1],
                               scale=2.0 if twice else 1.0).then_inc(work_drained, 1)

            def copy_sums(t):
                act.wait_ge(set_summed, NS * (t + 1))
                act.activation(partial[:, :, :], sum_bank[:, :], ACT.Copy).then_inc(sums_copied, 1)

            def copy_proj(t):
                act.wait_ge(work_filled, USES * t + PROJ + 1)
                if not is_tile(t, 0):
                    act.wait_ge(proj_ready, t)
                act.activation(proj[:, :, :], work_bank[PROJ % 2][:, :], ACT.Copy).then_inc(work_drained, 1)

            def sum_cross(t, p, l, c):
                act.wait_ge(crossed, count(2 * CH, t, CH * l + c + 1))
                products = cross_of(t)
                for o in range(OC * c, min(OC * c + OC, CUT if is_tile(t, T - 1) else O)):
                    last = act.activation(products[:, o, :], products[:, o, :], ACT.Relu,
                                          bias=bias12[:, O * l + o:O * l + o + 1],
                                          accum_out=mlp_in[p][:, O * (l + 1) + o:O * (l + 1) + o + 1])
                last.then_inc(cross_summed, 1)

            def mlp(t, p, k, part):
                act.wait_ge(mlp_pe, count(MP, t, part + 1))
                if part == 0:
                    act.activation(mlp_inT[:, :], mlp_inT_ps, ACT.Copy).then_inc(mlp_act, 1)
                elif part == 1:
                    for c in range(C1):
                        act.activation(hidden1[:, c, :], turn_bank[0][:, c * 128:(c + 1) * 128], ACT.Relu,
                                       bias=b1[:, c:c + 1]).then_inc(mlp_act, 1)
                elif part == 2:
                    for c in range(C2):
                        act.activation(hidden2[:, c, :], turn_bank[1][:, c * 128:(c + 1) * 128], ACT.Relu,
                                       bias=b2[:, c:c + 1]).then_inc(mlp_act, 1)
                else:
                    act.wait_ge(y_out[p], 16 * (k + 1))
                    act.activation(y_row[0:1, p, :], y_ps, ACT.Copy).then_inc(mlp_act, 1)
                    act.wait_ge(mlp_act, count(MA, t, MA))
                    act.dma_start(out[bass.ds(t * 128, 128), :].rearrange("b o -> o b"),
                                  y_row[0:1, p, :]).then_inc(y_out[p], 16)

            def step(t, p, k):
                q = 1 - p
                turn_copy(t + 1, q, 7)
                square(t, p, 3)
                relu_set(t, V2)
                relu_set(t, V3)
                sum_cross(t - 1, q, 1, 0)
                relu_set(t, DIAG)
                turn_copy(t + 1, q, 6)
                sum_cross(t - 1, q, 1, 1)
                turn_copy(t + 1, q, 5)
                relu_set(t, P0)
                square(t + 1, q, 0)
                turn_copy(t + 1, q, 4)
                sum_cross(t - 1, q, 1, 2)
                relu_set(t, V4)
                relu_set(t, P1)
                turn_copy(t + 1, q, 3)
                square(t + 1, q, 1)
                relu_set(t, V5)
                turn_copy(t + 1, q, 2)
                copy_sums(t)
                sum_cross(t - 1, q, 1, 3)
                turn_copy(t + 1, q, 1)
                turn_copy(t + 1, q, 0)
                square(t + 1, q, 2)
                mlp(t - 1, q, k, 0)
                sum_cross(t, p, 0, 0)
                mlp(t - 1, q, k, 1)
                sum_cross(t, p, 0, 1)
                relu_set(t + 1, V0)
                sum_cross(t, p, 0, 2)
                mlp(t - 1, q, k, 2)
                relu_set(t + 1, V1)
                sum_cross(t, p, 0, 3)
                copy_proj(t + 1)
                mlp(t - 1, q, k, 3)

            act.wait_ge(setup_pe, 1)
            act.wait_ge(const_vec, 1)
            for h in range(H):
                act.activation(WT[:, h, 0:O], work_bank[0][:, 48 * h:48 * h + O], ACT.Copy).then_inc(setup_act, 1)
                act.activation(WT[:, h, 2 * O:4 * O], work_bank[0][:, 48 * h + O:48 * h + 3 * O],
                               ACT.Copy).then_inc(setup_act, 1)
            for i in range(2):
                act.activation(bias0[:, i:i + 1], work_bank[0][:, 128:129], ACT.Copy,
                               scale=1.0 + i).then_inc(setup_act, 1)
            act.wait_ge(setup_act, 6)
            act.nop().then_inc(cross_summed, 2 * 2 * CH)
            act.nop().then_inc(mlp_act, 2 * MA)
            for p in range(2):
                act.nop().then_inc(y_out[p], 16)
            turn_copy(0, 0, 7)
            turn_copy(0, 0, 6)
            turn_copy(0, 0, 5)
            turn_copy(0, 0, 4)
            turn_copy(0, 0, 3)
            turn_copy(0, 0, 2)
            turn_copy(0, 0, 1)
            turn_copy(0, 0, 0)
            turn_copy(1, 1, 7)
            relu_set(0, V0)
            relu_set(0, V1)
            copy_proj(0)
            square(0, 0, 0)
            square(0, 0, 1)
            square(0, 0, 2)
            relu_set(0, V2)
            relu_set(0, V3)
            turn_copy(1, 1, 6)
            turn_copy(1, 1, 5)
            square(0, 0, 3)
            turn_copy(1, 1, 4)
            relu_set(0, DIAG)
            relu_set(0, P0)
            turn_copy(1, 1, 3)
            relu_set(0, V4)
            square(1, 1, 0)
            relu_set(0, P1)
            relu_set(0, V5)
            copy_sums(0)
            turn_copy(1, 1, 2)
            relu_set(1, V0)
            sum_cross(0, 0, 0, 0)
            turn_copy(1, 1, 1)
            turn_copy(1, 1, 0)
            sum_cross(0, 0, 0, 1)
            square(1, 1, 1)
            sum_cross(0, 0, 0, 2)
            relu_set(1, V1)
            sum_cross(0, 0, 0, 3)
            square(1, 1, 2)
            copy_proj(1)
            act.wait_ge(mlp_weights_in, 80)
            with act.Fori(0, (T - 2) // 2) as i:
                step(2 * i + 1, 1, i)
                step(2 * i + 2, 0, i)
            square(T - 1, 1, 3)
            relu_set(T - 1, V2)
            relu_set(T - 1, V3)
            relu_set(T - 1, DIAG)
            relu_set(T - 1, P0)
            relu_set(T - 1, V4)
            relu_set(T - 1, P1)
            relu_set(T - 1, V5)
            copy_sums(T - 1)
            sum_cross(T - 1, 1, 0, 0)
            sum_cross(T - 1, 1, 0, 1)
            mlp(T - 2, 0, (T - 2) // 2, 0)
            sum_cross(T - 1, 1, 0, 2)
            mlp(T - 2, 0, (T - 2) // 2, 1)
            sum_cross(T - 1, 1, 1, 0)
            sum_cross(T - 1, 1, 1, 1)
            mlp(T - 2, 0, (T - 2) // 2, 2)
            sum_cross(T - 1, 1, 1, 2)
            mlp(T - 2, 0, (T - 2) // 2, 3)
            mlp(T - 1, 1, (T - 2) // 2, 0)
            mlp(T - 1, 1, (T - 2) // 2, 1)
            mlp(T - 1, 1, (T - 2) // 2, 2)
            mlp(T - 1, 1, (T - 2) // 2, 3)
            for p in range(2):
                act.wait_ge(y_out[p], 16 * (T // 2 + 1))

        @block.tensor
        def _(pe):
            def turn(t, p, n):
                m = NP - 1 - n
                for f in (2 * n + 1, 2 * n):
                    pe.wait_ge(gathered[f], 16 * (t + 1))
                if not (is_tile(t, 0) and m < 2):
                    pe.wait_ge(xt_ready, NP * t + m - 1)
                if m < 2 and not is_tile(t, 0):
                    pe.wait_ge(mlp_act, count(MA, t - 3, 1 + C1 if m == 0 else MA))
                for i in range(2):
                    for h in range(H):
                        last = pe.transpose(turn_bank[m % 2][:, HB * i + 128 * h:HB * i + 128 * h + 128],
                                            X[p][:, 2 * n + i, 128 * h:128 * h + 128], ident[:, :])
                last.then_inc(turned, 1)

            def operand(t, p, m):
                n = OPERANDS[m]
                if m >= 2:
                    pe.wait_ge(vec_done, NV * t + freed_after[m - 2])
                elif not is_tile(t, 0):
                    pe.wait_ge(vec_done, NV * (t - 1) + freed_after[NOP - 2 + m])
                    if is_tile(t, 1) and m == 1:
                        pe.wait_ge(early_done, 1)
                for f in (2 * n, 2 * n + 1):
                    pe.wait_ge(gathered[f], 16 * (t + 1))
                for i in range(2):
                    for h in range(H):
                        last = pe.transpose(
                            operand_bank[m % 2][:, HB * i + 128 * h:HB * i + 128 * h + 128],
                            X[p][:, 2 * n + i, 128 * h:128 * h + 128], ident[:, :])
                last.then_inc(operand_ready, 1)

            def wait_work_bank(t, u):
                if not (is_tile(t, 0) and u < 2):
                    pe.wait_ge(work_drained, USES * t + u - 1)

            def contract(t, u):
                wait_work_bank(t, u)
                n, groups = SETS[u]
                for kind in ("v", "p", "d"):
                    need = max([begin + n for k, begin in groups if k == kind], default=0)
                    if need and kind == "v":
                        done = segments_before(need)
                        if is_tile(t, T - 1) and done > LATE:
                            pe.wait_ge(pool_done, NPOOL * T + 1)
                            done = LATE
                        pe.wait_ge(vec_done, NV * t + done)
                    elif need and kind == "p":
                        pe.wait_ge(pool_done, NPOOL * t + pool_rows_before(need))
                    elif need:
                        pe.wait_ge(squared, SQUARES * (t + 1))
                for h in range(H):
                    for j, (kind, slot) in enumerate(groups):
                        if kind == "v" and slot >= RING_1:
                            slot -= RING_1
                        src = {"v": vec_pairs, "p": pool_pairs, "d": squares}[kind]
                        last = pe.matmul(work_bank[u % 2][32 * j:32 * j + 32, 0:128 * n], WT[:, h, 0:32],
                                         src[:, slot:slot + n, 128 * h:128 * h + 128],
                                         start=(h == 0), stop=(h == H - 1))
                last.then_inc(work_filled, 1)

            def add_sets(t, n):
                uses = ORDER[4 * n:4 * n + 4]
                pe.wait_ge(work_drained, USES * t + uses[-1] + 1)
                if n == 0 and not is_tile(t, 0):
                    pe.wait_ge(z0_kept, count(1, t - 1, 1))
                for u in uses:
                    s = ORDER.index(u)
                    j = s % 4
                    cols = 128 * SETS[u][0]
                    pe.matmul(sum_bank[32 * j:32 * j + 32, 0:cols], pick_in_32[:, :], relued[:, s % RELUED, 0:cols],
                              start=(s < 4), stop=(s + 4 >= NS)).then_inc(set_summed, 1)

            def project(t, p):
                wait_work_bank(t, PROJ)
                pe.wait_ge(xt_ready, NP * (t + 1))
                for h in range(H):
                    for j in range(4):
                        last = pe.matmul(work_bank[PROJ % 2][32 * j:32 * j + 32, :], WT[:, h, 32:64],
                                         XT[p][:, 4 * j:4 * j + 4, 128 * h:128 * h + 128],
                                         start=(h == 0), stop=(h == H - 1))
                last.then_inc(work_filled, 1)

            def turn_proj(t):
                pe.wait_ge(work_drained, USES * t + PROJ + 1)
                pe.wait_ge(crossed, count(2 * CH, t - 1, 2 * CH))
                for i in range(4):
                    last = pe.transpose(proj_bank[:, 128 * i:128 * i + 128], proj[:, i, :], ident[:, :])
                last.then_inc(proj_ready, 1)

            def finish_z0(t):
                pe.wait_ge(sums_copied, t + 1)
                pe.wait_ge(z0_kept, count(1, t - 1, 1))
                for k in range(4):
                    last = pe.matmul(z0_ps, partial[:, k, :], pick_in_32[:, 0:O], start=(k == 0), stop=(k == 3))
                last.then_inc(z0_ready, 1)

            def mlp(t, p, k, part):
                if part == 0:
                    pe.wait_ge(cross_summed, count(2 * CH, t, 2 * CH))
                    pe.wait_ge(z0_kept, count(1, t, 1))
                    pe.wait_ge(xt_ready, NP * T if is_tile(t, T - 2, T - 1) else NP * (t + 3))
                    if is_tile(t, T - 1):
                        pe.wait_ge(mlp_act, count(MA, t - 1, MA))
                    pe.wait_ge(dense_in[p], 16 * (k + 1))
                    pe.matmul(mlp_inT_ps, mlp_in[p][:, :], ident[:, :], start=True, stop=True).then_inc(mlp_pe, 1)
                elif part == 1:
                    pe.wait_ge(mlp_act, count(MA, t, 1))
                    for c in range(C1):
                        last = pe.matmul(turn_bank[0][:, c * 128:(c + 1) * 128], w1[:, c, :], mlp_inT[:, :],
                                         start=True, stop=True)
                    last.then_inc(mlp_pe, 1)
                elif part == 2:
                    for m in range(C2):
                        for c in range(C1):
                            if m == 0:
                                pe.wait_ge(mlp_act, count(MA, t, 1 + c + 1))
                            last = pe.matmul(turn_bank[1][:, m * 128:(m + 1) * 128], w2[:, c, m * 128:(m + 1) * 128],
                                             hidden1[:, c, :], start=(c == 0), stop=(c == C1 - 1))
                    last.then_inc(mlp_pe, 1)
                else:
                    pe.wait_ge(mlp_act, count(MA, t, 1 + C1 + C2))
                    for m in range(C2):
                        last = pe.matmul(y_ps, w3[:, m:m + 1], hidden2[:, m, :],
                                         start=(m == 0), stop=(m == C2 - 1))
                    last.then_inc(mlp_pe, 1)

            def step(t, p, k):
                q = 1 - p
                turn(t + 1, q, 7)
                operand(t, p, 5)
                contract(t, V2)
                turn(t + 1, q, 6)
                contract(t, V3)
                operand(t + 1, q, 0)
                contract(t, DIAG)
                turn(t + 1, q, 5)
                contract(t, P0)
                contract(t, V4)
                operand(t + 1, q, 1)
                turn(t + 1, q, 4)
                add_sets(t, 0)
                turn(t + 1, q, 3)
                contract(t, P1)
                operand(t + 1, q, 2)
                turn_proj(t)
                contract(t, V5)
                operand(t + 1, q, 3)
                add_sets(t, 1)
                turn(t + 1, q, 2)
                add_sets(t, 2)
                turn(t + 1, q, 1)
                turn(t + 1, q, 0)
                finish_z0(t)
                contract(t + 1, V0)
                mlp(t - 1, q, k, 0)
                operand(t + 1, q, 4)
                mlp(t - 1, q, k, 1)
                contract(t + 1, V1)
                mlp(t - 1, q, k, 2)
                project(t + 1, q)
                mlp(t - 1, q, k, 3)

            pe.wait_ge(const_pool, 2)
            pe.wait_ge(const_vec, 1)
            pe.wait_ge(weights_in, 48)
            for h in range(H):
                pe.transpose(work_bank[0][:, 48 * h:48 * h + 48], layer_rows[:, 128 * h:128 * h + 128],
                             ident[0:L * O, 0:L * O])
            pe.matmul(work_bank[0][:, 128:129], spread32[:, :, :], bias_in[:, :], start=True,
                      stop=True).then_inc(setup_pe, 1)
            pe.nop().then_inc(mlp_pe, 2 * MP)
            pe.wait_ge(setup_act, 6)
            turn(0, 0, 7)
            turn(0, 0, 6)
            operand(0, 0, 0)
            turn(0, 0, 5)
            operand(0, 0, 1)
            turn(0, 0, 4)
            operand(0, 0, 2)
            turn(0, 0, 3)
            turn(0, 0, 2)
            operand(0, 0, 3)
            turn(0, 0, 1)
            turn(0, 0, 0)
            contract(0, V0)
            turn(1, 1, 7)
            contract(0, V1)
            project(0, 0)
            operand(0, 0, 4)
            operand(0, 0, 5)
            contract(0, V2)
            turn_proj(0)
            contract(0, V3)
            turn(1, 1, 6)
            operand(1, 1, 0)
            turn(1, 1, 5)
            turn(1, 1, 4)
            add_sets(0, 0)
            operand(1, 1, 1)
            contract(0, DIAG)
            turn(1, 1, 3)
            operand(1, 1, 2)
            contract(0, P0)
            contract(0, V4)
            contract(0, P1)
            contract(0, V5)
            operand(1, 1, 3)
            add_sets(0, 1)
            add_sets(0, 2)
            turn(1, 1, 2)
            turn(1, 1, 1)
            finish_z0(0)
            contract(1, V0)
            turn(1, 1, 0)
            contract(1, V1)
            operand(1, 1, 4)
            project(1, 1)
            pe.wait_ge(mlp_weights_in, 80)
            with pe.Fori(0, (T - 2) // 2) as i:
                step(2 * i + 1, 1, i)
                step(2 * i + 2, 0, i)
            operand(T - 1, 1, 5)
            contract(T - 1, V2)
            contract(T - 1, V3)
            contract(T - 1, DIAG)
            contract(T - 1, P0)
            contract(T - 1, V4)
            contract(T - 1, P1)
            add_sets(T - 1, 0)
            contract(T - 1, V5)
            add_sets(T - 1, 1)
            add_sets(T - 1, 2)
            mlp(T - 2, 0, (T - 2) // 2, 0)
            turn_proj(T - 1)
            finish_z0(T - 1)
            mlp(T - 2, 0, (T - 2) // 2, 1)
            mlp(T - 2, 0, (T - 2) // 2, 2)
            mlp(T - 2, 0, (T - 2) // 2, 3)
            mlp(T - 1, 1, (T - 2) // 2, 0)
            mlp(T - 1, 1, (T - 2) // 2, 1)
            mlp(T - 1, 1, (T - 2) // 2, 2)
            mlp(T - 1, 1, (T - 2) // 2, 3)

        @block.vector
        def _(vec):
            def segments(t, p, begin, end):
                for seg in vec_segments[begin:end + 1]:
                    f, g, n, slot, _ = seg
                    m = OPERANDS.index(f // 2)
                    vec.wait_ge(operand_ready, NOP * t + m + 1)
                    vec.wait_ge(xt_ready, NP * t + NP - (g // 2))
                    back, use = ring_guard(seg)
                    if use is not None and not (is_tile(t, 0) and back):
                        vec.wait_ge(work_filled, USES * (t - back) + use + 1)
                    col = HB * (f % 2)
                    vec.tensor_tensor(vec_pairs[:, slot:slot + n, :],
                                      operand_bank[m % 2][:, None, col:col + HB].to_broadcast([128, n, HB]),
                                      XT[p][:, g:g + n, :], ALU.mult).then_inc(vec_done, 1)

            def early_row():
                f, g, n = POOL_ROWS[EARLY]
                m, col = OPERANDS.index(f // 2), HB * (f % 2)
                vec.wait_ge(operand_ready, m + 1)
                vec.wait_ge(xt_ready, NP - g // 2)
                vec.tensor_tensor(pool_pairs[:, POOL_PAIRS - n:POOL_PAIRS, :],
                                  operand_bank[m % 2][:, None, col:col + HB].to_broadcast([128, n, HB]),
                                  XT[0][:, g:g + n, :], ALU.mult).then_inc(early_done, 1)

            def keep_z0(t, p):
                vec.wait_ge(z0_ready, t + 1)
                vec.wait_ge(mlp_pe, count(MP, t - 2, 1))
                vec.tensor_copy(mlp_in[p][:, 0:O], z0_ps).then_inc(z0_kept, 1)

            def cross_products(t, p, l, c):
                if l == 0:
                    vec.wait_ge(z0_kept, count(1, t, 1))
                    vec.wait_ge(proj_ready, t + 1)
                    if is_tile(t, T - 1):
                        vec.wait_ge(operand_ready, NOP * (T - 1))
                        vec.wait_ge(turned, NP * (T - 1))
                    else:
                        vec.wait_ge(cross_summed, count(2 * CH, t - 1, CH + c + 1))
                else:
                    vec.wait_ge(cross_summed, count(2 * CH, t, CH))
                z = mlp_in[p][:, None, O * l:O * l + O, None].to_broadcast([128, OC, O, F])
                P = proj_bank[:, :].rearrange("p (x l o) -> p l o x", l=2, o=O)
                vec.tensor_tensor(cross_of(t)[:, OC * c:OC * c + OC, :].rearrange("p o (g x) -> p o g x", x=F),
                                  z, P[:, l, OC * c:OC * c + OC, None, :].to_broadcast([128, OC, O, F]),
                                  ALU.mult).then_inc(crossed, 1)

            def sum_cross(t, p, l, c, begin):
                vec.wait_ge(crossed, count(2 * CH, t, CH * l + c + 1))
                products = cross_of(t)
                for o in range(begin, OC * c + OC):
                    last = vec.scalar_tensor_tensor(
                        out=products[:, o, :], in0=products[:, o, :], scalar=bias12[:, O * l + o:O * l + o + 1],
                        in1=zero.to_broadcast([128, F * F]), op0=ALU.add, op1=ALU.max,
                        accum_out=mlp_in[p][:, O * (l + 1) + o:O * (l + 1) + o + 1])
                last.then_inc(cross_summed, 1)

            def step(t, p, k):
                q = 1 - p
                segments(t, p, 0, 5)
                keep_z0(t - 1, q)
                cross_products(t - 1, q, 0, 0)
                segments(t, p, 6, 6)
                cross_products(t - 1, q, 0, 1)
                segments(t, p, 7, 7)
                cross_products(t - 1, q, 0, 2)
                segments(t, p, 8, 8)
                cross_products(t - 1, q, 0, 3)
                segments(t, p, 9, 9)
                cross_products(t - 1, q, 1, 0)
                segments(t, p, 10, 10)
                cross_products(t - 1, q, 1, 1)
                segments(t, p, 11, 11)
                cross_products(t - 1, q, 1, 2)
                cross_products(t - 1, q, 1, 3)

            vec.memset(WT[:, :, :], 0.0).then_inc(setup_vec, 1)
            vec.wait_ge(const_pool, 2)
            vec.tensor_reduce(pick_in_32[:, :], ident[:, :].rearrange("p (j c) -> p c j", c=32),
                              AX.X, ALU.add).then_inc(setup_vec, 1)
            vec.tensor_copy(spread32[:, :, :], ident[0:O, None, 0:32].to_broadcast([O, 4, 32])).then_inc(setup_vec, 1)
            vec.wait_ge(setup_vec, 3)
            vec.nop().then_inc(const_vec, 1)
            vec.nop().then_inc(z0_kept, 2)
            vec.nop().then_inc(crossed, 2 * 2 * CH)
            segments(0, 0, 0, 11)
            early_row()
            with vec.Fori(0, (T - 2) // 2) as i:
                step(2 * i + 1, 1, i)
                step(2 * i + 2, 0, i)
            segments(T - 1, 1, 0, 5)
            keep_z0(T - 2, 0)
            segments(T - 1, 1, 6, 6)
            cross_products(T - 2, 0, 0, 0)
            cross_products(T - 2, 0, 0, 1)
            segments(T - 1, 1, 7, 7)
            cross_products(T - 2, 0, 0, 2)
            segments(T - 1, 1, 8, 8)
            cross_products(T - 2, 0, 0, 3)
            segments(T - 1, 1, 9, 10)
            cross_products(T - 2, 0, 1, 0)
            cross_products(T - 2, 0, 1, 1)
            cross_products(T - 2, 0, 1, 2)
            sum_cross(T - 2, 0, 1, 0, OC * 0)
            cross_products(T - 2, 0, 1, 3)
            sum_cross(T - 2, 0, 1, 1, OC * 1)
            sum_cross(T - 2, 0, 1, 2, OC * 2)
            sum_cross(T - 2, 0, 1, 3, OC * 3)
            keep_z0(T - 1, 1)
            cross_products(T - 1, 1, 0, 0)
            cross_products(T - 1, 1, 0, 1)
            cross_products(T - 1, 1, 0, 2)
            cross_products(T - 1, 1, 0, 3)
            sum_cross(T - 1, 1, 0, CH - 1, CUT)
            cross_products(T - 1, 1, 1, 0)
            cross_products(T - 1, 1, 1, 1)
            cross_products(T - 1, 1, 1, 2)
            cross_products(T - 1, 1, 1, 3)
            sum_cross(T - 1, 1, 1, CH - 1, CUT)


_TABLES = [f"tbl_{f}" for f in range(16)]
_INS = ["dense_ctx", "ids"] + _TABLES + ["W_top1", "b_top1", "W_top2", "b_top2", "W_top3", "L0_rec_Ws", "L0_rec_bs"]
_OUTS = [((1024, 1), "float32")]


def kernel(**inputs):
    import numpy as _np
    import concourse.bacc as _bacc
    from concourse import mybir as _mybir
    from concourse.bass_utils import run_bass_kernel_spmd as _run

    nc = _bacc.Bacc("TRN2", target_bir_lowering=False, num_devices=1)
    arrays, args = {}, {}
    for name in _INS:
        a = _np.ascontiguousarray(inputs[name])
        arrays[f"in_{name}"] = a
        args[name] = nc.dram_tensor(f"in_{name}", a.shape, _mybir.dt.from_np(a.dtype), kind="ExternalInput").ap()
    shape, dtype = _OUTS[0]
    y = nc.dram_tensor("out_y", shape, _mybir.dt.from_np(_np.dtype(dtype)), kind="ExternalOutput").ap()
    dlrm_tower(nc, args["dense_ctx"], args["ids"], [args[n] for n in _TABLES], args["W_top1"], args["b_top1"],
               args["W_top2"], args["b_top2"], args["W_top3"], args["L0_rec_Ws"], args["L0_rec_bs"], y)
    r = _run(nc, [arrays], core_ids=[0])
    return r.results[0]["out_y"]
```
